# Optimizing a Trainium2 kernel written in Bass

```python
import numpy as np
import jax
import jax.numpy as jnp

def _softmax(x, axis=-1):
    return jax.nn.softmax(x, axis=axis)

def _gelu(x):
    return jax.nn.gelu(x, approximate=True)

def _silu(x):
    return jax.nn.silu(x)

def _sigmoid(x):
    return jax.nn.sigmoid(x)

def _layernorm(x, axis=-1, eps=1e-05):
    m = jnp.mean(x, axis=axis, keepdims=True)
    v = jnp.var(x, axis=axis, keepdims=True)
    return (x - m) / jnp.sqrt(v + eps)

def _scatter_add(tgt, idx, src, axis=0):
    return tgt.at[idx].add(src)

def _segment_sum(src, seg, n):
    return jax.ops.segment_sum(src, seg, n)
kernel_name = 'mk_adj_preln_d2_adj_r2_20bb8a'

def setup_inputs(seed: int=0):
    np.random.seed(seed)
    _w = jnp.asarray

    def _rec_inputs():
        import jax
        import jax.numpy as jnp
        _gk = jax.random.key(seed)
        x = -0.0002928 + 1 * jax.random.normal(jax.random.fold_in(_gk, 1), (8, 1024, 128), jnp.float32)
        _a = jax.random.bernoulli(jax.random.fold_in(_gk, 2), 0.00195312, (1024, 1024))
        _a = jnp.logical_or(_a, jnp.swapaxes(_a, -1, -2))
        _a = jnp.logical_or(_a, jnp.eye(1024, dtype=bool))
        _af = _a.astype(jnp.float32)
        _af = _af * jax.random.uniform(jax.random.fold_in(_gk, 3), (1024, 1024), jnp.float32, 0.05, 1)
        adj = _af
        return (x, adj)
    x, adj = _rec_inputs()

    def _L0_gnn_setup():
        import jax, jax.numpy as jnp
        import numpy as np
        B, N, F_IN, F_OUT, K = (16, 1024, 128, 128, 3)

        def _scaled_laplacian(adj):
            n = adj.shape[0]
            A = adj * (1.0 - jnp.eye(n, dtype=adj.dtype))
            deg = A.sum(axis=1)
            safe = jnp.where(deg > 0, deg, 1.0)
            dinv = jnp.where(deg > 0, 1.0 / jnp.sqrt(safe), 0.0)
            return -(dinv[:, None] * A * dinv[None, :])
        key = jax.random.key(seed)
        k1, k2, k3, _ = jax.random.split(key, 4)
        x = jax.random.normal(k1, (B, N, F_IN), dtype=jnp.float32)
        adj = jax.random.uniform(k2, (N, N), dtype=jnp.float32)
        Ws = jax.random.normal(k3, (K, F_IN, F_OUT), dtype=jnp.float32) / np.float32(np.sqrt(F_IN))
        bias = jnp.zeros((F_OUT,), dtype=jnp.float32)
        return {'x': x, 'adj': adj, 'Ws': Ws, 'bias': bias}
    _L0_gnn_all = _L0_gnn_setup()
    _L0_gnn_in = {k: v for k, v in _L0_gnn_all.items() if k in ('Ws', 'bias')}
    del _L0_gnn_all

    def _L1_gnn_setup():
        import jax, jax.numpy as jnp
        import numpy as np
        from jax import lax
        CONV_ORDER = 3

        def _chebyshev(adj, x, order):

            def step(carry, _):
                nxt = jnp.einsum('ij,bjc->bic', adj, carry)
                return (nxt, nxt)
            _, xs = lax.scan(step, x, None, length=order)
            return jnp.moveaxis(xs, 0, -1)
        key = jax.random.key(seed)
        k1, k2, k3, k4 = jax.random.split(key, 4)
        B, E, C_in, C_out, K, n_adjs = (8, 2048, 128, 128, CONV_ORDER, 2)
        x_1 = jax.random.normal(k1, (B, E, C_in), dtype=jnp.float32)
        adj0 = jax.random.normal(k2, (E, E), dtype=jnp.float32) / np.sqrt(E)
        adj1 = jax.random.normal(k3, (E, E), dtype=jnp.float32) / np.sqrt(E)
        kdim = K * n_adjs + 1
        std = 1.414 * np.sqrt(2.0 / float((C_in + C_out) * kdim))
        weight_1 = std * jax.random.normal(k4, (C_in, C_out, kdim), dtype=jnp.float32)
        return {'x_1': x_1, 'adj0': adj0, 'adj1': adj1, 'weight_1': weight_1}
    _L1_gnn_all = _L1_gnn_setup()
    _L1_gnn_in = {k: v for k, v in _L1_gnn_all.items() if k in ('weight_1',)}
    del _L1_gnn_all
    return {'x': x, 'adj': adj, 'L0_gnn_Ws': _L0_gnn_in['Ws'], 'L0_gnn_bias': _L0_gnn_in['bias'], 'L1_gnn_weight_1': _L1_gnn_in['weight_1']}

def reference(x, adj, L0_gnn_Ws, L0_gnn_bias, L1_gnn_weight_1):
    import jax
    import jax.numpy as jnp

    def _L0_gnn_ref(x, adj, Ws, bias):
        import jax, jax.numpy as jnp
        import numpy as np
        B, N, F_IN, F_OUT, K = (16, 1024, 128, 128, 3)

        def _scaled_laplacian(adj):
            n = adj.shape[0]
            A = adj * (1.0 - jnp.eye(n, dtype=adj.dtype))
            deg = A.sum(axis=1)
            safe = jnp.where(deg > 0, deg, 1.0)
            dinv = jnp.where(deg > 0, 1.0 / jnp.sqrt(safe), 0.0)
            return -(dinv[:, None] * A * dinv[None, :])
        L = _scaled_laplacian(adj)
        Tx0 = x
        out = jnp.einsum('bnf,fo->bno', Tx0, Ws[0])
        Tx1 = jnp.einsum('mn,bnf->bmf', L, Tx0)
        out = out + jnp.einsum('bnf,fo->bno', Tx1, Ws[1])
        for k in range(2, K):
            Tx2 = 2.0 * jnp.einsum('mn,bnf->bmf', L, Tx1) - Tx0
            out = out + jnp.einsum('bnf,fo->bno', Tx2, Ws[k])
            Tx0, Tx1 = (Tx1, Tx2)
        return out + bias

    def _L1_gnn_ref(x_1, adj0, adj1, weight_1):
        import jax, jax.numpy as jnp
        import numpy as np
        from jax import lax
        CONV_ORDER = 3

        def _chebyshev(adj, x, order):

            def step(carry, _):
                nxt = jnp.einsum('ij,bjc->bic', adj, carry)
                return (nxt, nxt)
            _, xs = lax.scan(step, x, None, length=order)
            return jnp.moveaxis(xs, 0, -1)
        parts = [x_1[..., None], _chebyshev(adj0, x_1, CONV_ORDER), _chebyshev(adj1, x_1, CONV_ORDER)]
        x_all = jnp.concatenate(parts, axis=3)
        y_1 = jnp.einsum('bnik,iok->bno', x_all, weight_1)
        return y_1
    h = jnp.maximum(_layernorm(x, axis=-1), 0.0)
    x = x + _L0_gnn_ref(h, adj, L0_gnn_Ws, L0_gnn_bias)
    h = jnp.maximum(_layernorm(x, axis=-1), 0.0)
    x = x + _L1_gnn_ref(h, adj, adj, L1_gnn_weight_1)
    return x

_drawn_inputs = setup_inputs


def setup_inputs(seed=0):
    import zlib

    import numpy as np

    out = dict(_drawn_inputs(seed))
    spreads = {'L0_gnn_bias': (0.0, 0.1)}
    factors = {}
    for name, (base, spread) in spreads.items():
        noise = np.random.default_rng([zlib.crc32(name.encode()), seed]).standard_normal(out[name].shape)
        drawn = base * np.exp(spread * noise) if base else spread * noise
        out[name] = jnp.asarray(drawn.astype(out[name].dtype))
    for name, factor in factors.items():
        out[name] = (out[name] * factor).astype(out[name].dtype)
    return out
```

```python
from contextlib import ExitStack

import concourse.bass as bass
from concourse import mybir

F32 = mybir.dt.float32
F16 = mybir.dt.float16
I32 = mybir.dt.int32
ALU = mybir.AluOpType
ACT = mybir.ActivationFunctionType
AX = mybir.AxisListType
ABSMAX = bass.bass_isa.ReduceOp.absmax

P = 128
EXPONENT = 0x7F800000
TINY = 2.0 ** -100
PART = 2.0 ** 14
H_SCALE = 2.0 ** 11
EPS = 1e-5


def build(nc, x, adj, w0, bias, w1, out):
    B, N, F = x.shape
    M = N // P
    HB = B // 2
    HC = HB * F
    NB = [3, 4]
    PAIRS = M // 2
    DIAG = N + P
    J1 = 2 * M

    x_t = x.rearrange("b (m p) f -> m p b f", p=P)
    out_t = out.rearrange("b (m p) f -> m p b f", p=P)
    adj_t = adj.rearrange("(m p) n -> m p n", p=P)

    with ExitStack() as ctx:
        def sb(name, shape, dt=F32):
            return ctx.enter_context(nc.sbuf_tensor(name, shape, dt))

        def sem(name):
            return ctx.enter_context(nc.semaphore(name))

        G = sb("G", [P, 3, M, B * F])
        work = sb("work", [P, M * HC])
        stage = [work[:, u * N:(u + 1) * N] for u in range(2)]
        As = [work[:, (2 + u) * N:(3 + u) * N] for u in range(2)]
        G3 = work[:, :].rearrange("p (m n) -> p m n", m=M)
        Zh = sb("Zh", [P, 2, M, HC], F16)
        Zl = sb("Zl", [P, 2, M, HC], F16)
        ATh_all = sb("ATh", [P, M * DIAG], F16)
        ATl_all = sb("ATl", [P, M * DIAG], F16)
        ATh, ATl = (t[:, 0:M * N].rearrange("p (k m) -> p k m", k=M) for t in (ATh_all, ATl_all))
        ATh_diag, ATl_diag = (t[:, :].rearrange("p (k m) -> p k m", m=DIAG)[:, :, 0:P]
                              for t in (ATh_all, ATl_all))
        ADh = sb("ADh", [P, M, P], F16)
        ADl = sb("ADl", [P, M, P], F16)
        Dg = [sb(f"Dg{u}", [P, P]) for u in range(2)]
        xn = [sb(f"xn{u}", [P, HC]) for u in range(2)]
        hTh = [sb(f"hTh{u}", [P, HC], F16) for u in range(2)]
        hTl = [sb(f"hTl{u}", [P, HC], F16) for u in range(2)]
        w0_in = sb("w0_in", [P, 3, F])
        w1_in = sb("w1_in", [P, F, 7])
        wcat = [w0_in, sb("w1_cat", [P, 4, F])]
        Wh = [sb(f"Wh{i}", [P, NB[i] * F], F16) for i in range(2)]
        Wl = [sb(f"Wl{i}", [P, NB[i] * F], F16) for i in range(2)]
        ident = sb("ident", [P, P])
        offdiag = sb("offdiag", [P, P])
        bias_b = sb("bias_b", [P, F])
        junk = Zl[:, 1, 0:N // HC, :].rearrange("p m n -> p (m n)")

        bn6 = [sb(f"bn6_{u}", [P, HB, 6]) for u in range(2)]
        moments = [sb(f"moments{u}", [P, HB, 2]) for u in range(2)]
        var = [sb(f"var{u}", [P, HB]) for u in range(2)]
        sd = [sb(f"sd{u}", [P, HB]) for u in range(2)]
        r0 = [sb(f"r0_{u}", [P, HB]) for u in range(2)]
        nt = [sb(f"nt{u}", [P, HB]) for u in range(2)]
        rstd = [sb(f"rstd{u}", [P, HB]) for u in range(2)]
        wmax = sb("wmax", [P, 2])
        wgmax = sb("wgmax", [P, 2])
        wscale = sb("wscale", [P, 2])
        wback = sb("wback", [P, 2])
        amax = [sb(f"amax{u}", [P, 1]) for u in range(2)]
        ascale = [sb(f"ascale{u}", [P, 1]) for u in range(2)]
        aback = sb("aback", [P, 2, M])
        rowsum = sb("rowsum", [P, M])
        dvec = sb("dvec", [P, 2, M])
        dt = [sb(f"dt{i}", [P, M]) for i in range(8)]
        tmax = sb("tmax", [P, 2, M])
        dmax = sb("dmax", [P, 2, M])
        hmax = sb("hmax", [P, 2])
        hgmax = sb("hgmax", [P, 2])
        zscale = sb("zscale", [P, 2, M])
        zback = sb("zback", [P, 2])
        alpha = sb("alpha", [P, 2, M])
        pw = sb("pw", [P, 14, 3])

        psA = ctx.enter_context(nc.psum_tensor("psA", [P, 2, 512], F32))
        psT = ctx.enter_context(nc.psum_tensor("psT", [P, 2, 512], F32))
        psW = ctx.enter_context(nc.psum_tensor("psW", [P, HB, 512], F32))

        adj_in = [sem(f"adj_in{u}") for u in range(2)]
        x_in = [sem(f"x_in{u}") for u in range(2)]
        (w_in0, w_in1, bias_in, out_done, consts, w_combined, w_max, w_gmax, w_scale, w_hi, w_lo,
         pow2_step, a_max, a_scale, as_scaled, dg_copied, as_ready, a_sum, at_transposed, at_hi,
         at_done, dinv_step, deg_parts, ln_stats, ln_moments, ln_var, ln_sd, ln_r0, ln_n1, ln_n2, ln_n3,
         ln_rstd, xn_done, xT_done, hT_hi, hT_lo, hw_done, gcols_done, g0_done, bias_added,
         col_max, mm_done, bank_free, hm_step, half_max, half_gmax, scale_ready, z_hi, z_lo,
         diag_hi, diag_lo) = (sem(n) for n in (
            "w_in0 w_in1 bias_in out_done consts w_combined w_max w_gmax w_scale w_hi w_lo "
            "pow2_step a_max a_scale as_scaled dg_copied as_ready a_sum at_transposed at_hi "
            "at_done dinv_step deg_parts ln_stats ln_moments ln_var ln_sd ln_r0 ln_n1 ln_n2 ln_n3 "
            "ln_rstd xn_done xT_done hT_hi hT_lo hw_done gcols_done g0_done bias_added "
            "col_max mm_done bank_free hm_step half_max half_gmax scale_ready z_hi z_lo "
            "diag_hi diag_lo").split())

        def tile(j, c, m):
            return G[:, j, m, c * HC:(c + 1) * HC]

        def by_batch(ap):
            return ap.rearrange("p (b f) -> p b f", f=F)

        def last_of_chain(layer, c, m):
            return tile(2, c, m) if layer == 0 else G3[:, m, :]

        SOURCE = [lambda c, m: last_of_chain(0, c, m), lambda c, m: tile(1, c, m),
                  lambda c, m: last_of_chain(1, c, m), lambda c, m: tile(2, c, m), lambda c, m: tile(1, c, m)]
        TARGET = [1, 0, 2, 1, 0]
        LAYER = [0, 0, 1, 1, 1]

        block = ctx.enter_context(nc.Block())

        @block.sync
        def _(sp):
            sp.dma_start(w0_in[:, :, :], w0.rearrange("k i o -> i k o")).then_inc(w_in0, 16)
            sp.dma_start(bias_b[:, :], bias.partition_broadcast(P)).then_inc(bias_in, 16)
            with sp.Fori(0, PAIRS) as i:
                for u in range(2):
                    m = 2 * i + u
                    sp.wait_ge(x_in[u], 16 * i + 16)
                    sp.dma_start(by_batch(tile(0, 0, m)), x_t[m, :, 0:HB, :]).then_inc(x_in[u], 16)
                    sp.wait_ge(as_scaled, m + 1)
                    sp.dma_start(stage[u], adj_t[m, :, :]).then_inc(adj_in[u], 16)
            with sp.Fori(0, PAIRS) as i:
                for u in range(2):
                    sp.wait_ge(x_in[u], 16 * i + 16 * PAIRS + 16)
                    sp.dma_start(by_batch(tile(0, 1, 2 * i + u)), x_t[2 * i + u, :, HB:B, :]).then_inc(x_in[u], 16)
            sp.dma_start(w1_in[:, :, :], w1).then_inc(w_in1, 16)
            for c in range(2):
                with sp.Fori(0, M) as m:
                    sp.wait_ge(bank_free, m + (8 + c) * M + 3)
                    sp.dma_start(out_t[m, :, c * HB:(c + 1) * HB, :], by_batch(tile(0, c, m))).then_inc(out_done, 16)
            sp.wait_ge(out_done, 16 * 2 * M)

        @block.gpsimd
        def _(pool):
            nc.gpsimd.memset(ident[:, :], 0.0).then_inc(consts, 1)
            nc.gpsimd.memset(offdiag[:, :], 1.0).then_inc(consts, 1)
            pool.wait_ge(consts, 2)
            for t, v in ((ident, 1.0), (offdiag, 0.0)):
                nc.gpsimd.affine_select(out=t[:, :], in_=t[:, :], compare_op=ALU.not_equal, fill=v, base=0,
                                        pattern=[[-1, P]], channel_multiplier=1).then_inc(consts, 1)
            pool.wait_ge(consts, 4)
            pool.wait_ge(w_max, 1)
            nc.gpsimd.partition_all_reduce(wgmax[:, 0:1], wmax[:, 0:1], P, ABSMAX).then_inc(w_gmax, 1)

            def add_bias(j, c, m):
                pool.wait_ge(xn_done, j + 1)
                pool.nop(nofuse=True)
                nc.gpsimd.tensor_tensor(by_batch(tile(0, c, m)), by_batch(tile(0, c, m)), bias_b[:, :].unsqueeze(1).broadcast_to([P, HB, F]),
                                        ALU.add).then_inc(bias_added, 1)

            nc.gpsimd.memset(wgmax[:, 1:2], 0.0).then_inc(as_scaled, 2)
            pool.wait_ge(bias_in, 16)
            with pool.Fori(0, PAIRS) as i:
                for u in range(2):
                    m = 2 * i + u
                    pool.wait_ge(a_scale, m + 1)
                    pool.wait_ge(at_done, m + 1)
                    pool.nop(nofuse=True)
                    nc.gpsimd.tensor_scalar(As[u], stage[u], ascale[u][:, :], None, ALU.mult).then_inc(as_scaled, 1)
                    pool.wait_ge(as_scaled, m + 3)
                    own = As[u][:, bass.ts(m, P)]
                    nc.gpsimd.tensor_copy(Dg[u][:, :], own).then_inc(dg_copied, 1)
                    pool.wait_ge(dg_copied, m + 1)
                    pool.nop(nofuse=True)
                    nc.gpsimd.tensor_tensor(own, own, offdiag[:, :], ALU.mult).then_inc(as_ready, 1)
                    add_bias(m, 0, m)

            def reduce_half(q):
                pool.wait_ge(half_max, q + 1)
                c = q % 2
                nc.gpsimd.partition_all_reduce(hgmax[:, c:c + 1], hmax[:, c:c + 1], P, ABSMAX).then_inc(half_gmax, 1)

            reduce_half(0)
            with pool.Fori(0, M) as m:
                add_bias(m + M, 1, m)
            reduce_half(1)
            pool.wait_ge(w_max, 2)
            nc.gpsimd.partition_all_reduce(wgmax[:, 1:2], wmax[:, 1:2], P, ABSMAX).then_inc(w_gmax, 1)
            for q in range(2, 10):
                reduce_half(q)

        @block.scalar
        def _(act):
            def chain_sd(j, u):
                act.wait_ge(ln_var, j + 1)
                nc.scalar.activation(sd[u][:, :], var[u][:, :], ACT.Sqrt).then_inc(ln_sd, 1)

            def chain_hi(j, u):
                act.wait_ge(xT_done, j + 1)
                nc.scalar.activation(hTh[u][:, :], psT[:, 0, :], ACT.Relu).then_inc(hT_hi, 1)

            def chain_columns(j, layer, c, m):
                act.wait_ge(hw_done, j + 1)
                if layer == 1:
                    nc.scalar.activation(by_batch(G3[:, m, :]), psW[:, :, 3 * F:4 * F], ACT.Copy,
                                         scale=wback[:, 1:2])
                for k in (1, 2):
                    last = nc.scalar.activation(by_batch(tile(k, c, m)), psW[:, :, k * F:(k + 1) * F], ACT.Copy,
                                                scale=wback[:, layer:layer + 1])
                last.then_inc(gcols_done, 1)

            def weights_hi(layer):
                act.wait_ge(w_scale, layer + 1)
                nc.scalar.activation(Wh[layer][:, :], wcat[layer][:, :, :].rearrange("p k o -> p (k o)"), ACT.Copy,
                                     scale=wscale[:, layer:layer + 1]).then_inc(w_hi, 1)

            def split_hi(q):
                c = q % 2
                act.wait_ge(scale_ready, q + 1)
                with act.Fori(0, M) as m:
                    nc.scalar.activation(Zh[:, c, m, :], SOURCE[q // 2](c, m), ACT.Copy,
                                         scale=zscale[:, c, bass.ds(m, 1)]).then_inc(z_hi, 1)

            weights_hi(0)
            with act.Fori(0, PAIRS) as i:
                for u in range(2):
                    m = 2 * i + u
                    chain_sd(m, u)
                    act.wait_ge(as_ready, m + 1)
                    nc.scalar.activation(junk, As[u], ACT.Copy,
                                         accum_out=rowsum[:, bass.ds(m, 1)]).then_inc(a_sum, 1)
                    chain_hi(m, u)
                    act.wait_ge(at_transposed, m + 1)
                    nc.scalar.activation(ATh[:, :, bass.ts(m, P)], psA[:, :, :].rearrange("p a (k m) -> p (a k) m", m=P),
                                         ACT.Copy)
                    nc.scalar.activation(ADh[:, m, :], psT[:, 1, 0:P], ACT.Copy).then_inc(at_hi, 1)
                    chain_columns(m, 0, 0, m)
            act.wait_ge(dinv_step, 3)
            nc.scalar.activation(dt[3][:, :], dt[2][:, :], ACT.Sqrt).then_inc(dinv_step, 1)
            split_hi(0)
            with act.Fori(0, PAIRS) as i:
                for u in range(2):
                    j = 2 * i + u + M
                    chain_sd(j, u)
                    chain_hi(j, u)
                    chain_columns(j, 0, 1, 2 * i + u)
            split_hi(1)
            weights_hi(1)
            split_hi(2)
            split_hi(3)

            def follow(c, m, u, j):
                chain_hi(j, 1 - u)
                chain_sd(j + 1, u)
                chain_columns(j, 1, c, m)

            chain_sd(J1, 0)
            for c in range(2):
                if c == 1:
                    chain_hi(J1 + M - 1, 1)
                    chain_sd(J1 + M, 0)
                    chain_columns(J1 + M - 1, 1, 0, M - 1)
                    split_hi(4)
                with act.Fori(0, PAIRS - 1) as i:
                    for u in (1, 0):
                        m = 2 * i + (1 if u else 2)
                        follow(c, m - 1, u, m - 1 + J1 + c * M)
                follow(c, M - 2, 1, M - 2 + J1 + c * M)
            act.wait_ge(mm_done, 4 * M)
            nc.scalar.copy(ATh_diag, ADh[:, :, :]).then_inc(diag_hi, 1)
            chain_hi(J1 + 2 * M - 1, 1)
            chain_columns(J1 + 2 * M - 1, 1, 1, M - 1)
            for q in range(5, 10):
                split_hi(q)

        @block.tensor
        def _(pe):
            def products(q, m, bank, ks):
                c = q % 2
                for k in ks:
                    for a, z in ((ATh, Zh), (ATh, Zl), (ATl, Zh)):
                        last = nc.tensor.matmul(psA[:, bank, :], a[:, k, bass.ts(m, P)], z[:, c, k, :],
                                                start=(k == 0 and z is Zh and a is ATh),
                                                stop=(k == M - 1 and a is ATl))
                if ks[-1] == M - 1:
                    last.then_inc(mm_done, 1)

            def chain_transpose(j, u):
                pe.wait_ge(xn_done, j + 1)
                pe.wait_ge(hT_lo, j + 1)
                for b in range(HB):
                    last = nc.tensor.transpose(psT[:, 0, b * F:(b + 1) * F], xn[u][:, b * F:(b + 1) * F], ident[:, :])
                last.then_inc(xT_done, 1)

            def chain_weights(j, u, layer):
                pe.wait_ge(hT_lo, j + 2)
                pe.wait_ge(g0_done, j + 1)
                n = NB[layer] * F
                for b in range(HB):
                    for h, w in ((hTh, Wh), (hTh, Wl), (hTl, Wh)):
                        last = nc.tensor.matmul(psW[:, b, 0:n], h[u][:, b * F:(b + 1) * F], w[layer][:, :],
                                                start=(h is hTh and w is Wh), stop=(h is hTl))
                last.then_inc(hw_done, 1)

            def slot(q, m, bank, g, chain=()):
                pe.wait_ge(bank_free, g + 1)
                steps = [s for j, u, layer in chain for s in ((chain_transpose, (j, u)), (chain_weights, (j, u, layer)))]
                parts = max(len(steps), 1)
                for n in range(parts):
                    products(q, m, bank, list(range(n * M // parts, (n + 1) * M // parts)))
                    if steps:
                        steps[n][0](*steps[n][1])

            def half_ready(q):
                pe.wait_ge(z_lo, M * (q + 1))

            pe.wait_ge(consts, 4)
            pe.wait_ge(w_lo, 1)
            with pe.Fori(0, PAIRS) as i:
                for u in range(2):
                    m = 2 * i + u
                    chain_transpose(m, u)
                    pe.wait_ge(as_ready, m + 1)
                    pe.wait_ge(at_done, m + 2)
                    for k in range(M):
                        nc.tensor.transpose(psA[:, k // 4, (k % 4) * P:(k % 4 + 1) * P],
                                            As[u][:, k * P:(k + 1) * P], ident[:, :])
                    nc.tensor.transpose(psT[:, 1, 0:P], Dg[u][:, :], ident[:, :]).then_inc(at_transposed, 1)
                    chain_weights(m, u, 0)
            pe.wait_ge(at_done, M + 2)
            half_ready(0)
            with pe.Fori(0, PAIRS // 2) as i:
                for u in range(2):
                    m = 2 * i + u
                    slot(0, m, u, m, [(2 * m + M, 0, 0), (2 * m + M + 1, 1, 0)])
            with pe.Fori(0, PAIRS // 2) as i:
                for u in range(2):
                    m = 2 * i + u + M // 2
                    slot(0, m, u, m)
            half_ready(1)
            with pe.Fori(0, PAIRS) as i:
                for u in range(2):
                    slot(1, 2 * i + u, u, 2 * i + u + M)
            pe.wait_ge(w_lo, 2)
            for c in range(2):
                half_ready(2 + c)
                g0 = (2 + c) * M
                slot(2 + c, 0, 0, g0, [(J1 + M - 1, 1, 1)] if c else [])
                with pe.Fori(0, PAIRS - 1) as i:
                    for u in (1, 0):
                        m = 2 * i + (1 if u else 2)
                        slot(2 + c, m, u, m + g0, [(m - 1 + J1 + c * M, 1 - u, 1)])
                slot(2 + c, M - 1, 1, g0 + M - 1, [(M - 2 + J1 + c * M, 0, 1)])
            pe.wait_ge(diag_hi, 1)
            pe.wait_ge(diag_lo, 1)
            half_ready(4)
            slot(4, 0, 0, 4 * M, [(J1 + 2 * M - 1, 1, 1)])
            with pe.Fori(0, PAIRS - 1) as i:
                for u in (1, 0):
                    m = 2 * i + (1 if u else 2)
                    slot(4, m, u, m + 4 * M)
            slot(4, M - 1, 1, 5 * M - 1)
            for q in range(5, 10):
                half_ready(q)
                with pe.Fori(0, PAIRS) as i:
                    for u in range(2):
                        slot(q, 2 * i + u, u, 2 * i + u + q * M)

        @block.vector
        def _(dve):
            def power_of_two(src, n, call):
                t = pw[:, n, :]
                nc.vector.tensor_scalar(t[:, 0:1], src, TINY, None, ALU.max).then_inc(pow2_step, 1)
                dve.wait_ge(pow2_step, 3 * call + 1)
                nc.vector.tensor_scalar(t[:, 1:2].bitcast(I32), t[:, 0:1].bitcast(I32), EXPONENT, None,
                                        ALU.bitwise_and).then_inc(pow2_step, 1)
                dve.wait_ge(pow2_step, 3 * call + 2)
                nc.vector.reciprocal(t[:, 2:3], t[:, 1:2]).then_inc(pow2_step, 1)
                dve.wait_ge(pow2_step, 3 * call + 3)
                return t[:, 1:2], t[:, 2:3]

            def weights(layer):
                cat = wcat[layer][:, :, :].rearrange("p k o -> p (k o)")
                dve.wait_ge(w_combined, 2 * layer + 2)
                nc.vector.tensor_reduce(wmax[:, layer:layer + 1], cat, AX.X, ALU.max,
                                        apply_absolute_value=True).then_inc(w_max, 1)
                dve.wait_ge(w_gmax, layer + 1)
                p, rp = power_of_two(wgmax[:, layer:layer + 1], layer, layer * (M + 3))
                nc.vector.tensor_scalar(wback[:, layer:layer + 1], p, 1.0 / (PART * H_SCALE), None, ALU.mult)
                nc.vector.tensor_scalar(wscale[:, layer:layer + 1], rp, PART, None, ALU.mult).then_inc(w_scale, 1)
                dve.wait_ge(w_scale, layer + 1)
                dve.wait_ge(w_hi, layer + 1)
                nc.vector.scalar_tensor_tensor(Wl[layer][:, :], cat, wscale[:, layer:layer + 1], Wh[layer][:, :],
                                               ALU.mult, ALU.subtract).then_inc(w_lo, 1)

            def normalise(j, u, c, m):
                src = tile(0, c, m)
                dve.nop(nofuse=True)
                for b in range(HB):
                    last = nc.vector.bn_stats(bn6[u][:, b, :], src[:, b * F:(b + 1) * F])
                last.then_inc(ln_stats, 1)
                dve.wait_ge(ln_stats, j + 1)
                dve.nop(nofuse=True)
                for b in range(HB):
                    last = nc.vector.bn_aggr(moments[u][:, b, :], bn6[u][:, b, :])
                last.then_inc(ln_moments, 1)
                dve.wait_ge(ln_moments, j + 1)
                nc.vector.tensor_scalar(var[u][:, :], moments[u][:, :, 1], EPS, None, ALU.add).then_inc(ln_var, 1)
                dve.wait_ge(ln_sd, j + 1)
                nc.vector.reciprocal(r0[u][:, :], sd[u][:, :]).then_inc(ln_r0, 1)
                dve.wait_ge(ln_r0, j + 1)
                nc.vector.tensor_tensor(nt[u][:, :], r0[u][:, :], var[u][:, :], ALU.mult).then_inc(ln_n1, 1)
                dve.wait_ge(ln_n1, j + 1)
                nc.vector.tensor_tensor(nt[u][:, :], nt[u][:, :], r0[u][:, :], ALU.mult).then_inc(ln_n2, 1)
                dve.wait_ge(ln_n2, j + 1)
                nc.vector.tensor_scalar(nt[u][:, :], nt[u][:, :], -0.5 * H_SCALE, 1.5 * H_SCALE, ALU.mult,
                                        ALU.add).then_inc(ln_n3, 1)
                dve.wait_ge(ln_n3, j + 1)
                nc.vector.tensor_tensor(rstd[u][:, :], nt[u][:, :], r0[u][:, :], ALU.mult).then_inc(ln_rstd, 1)
                dve.wait_ge(ln_rstd, j + 1)
                for b in range(HB):
                    last = nc.vector.tensor_scalar(xn[u][:, b * F:(b + 1) * F], src[:, b * F:(b + 1) * F],
                                                   moments[u][:, b, 0:1], rstd[u][:, b:b + 1],
                                                   ALU.subtract, ALU.mult)
                last.then_inc(xn_done, 1)

            def chain_lo(j, u):
                dve.wait_ge(hT_hi, j + 1)
                nc.vector.scalar_tensor_tensor(hTl[u][:, :], psT[:, 0, :], 0.0, hTh[u][:, :],
                                               ALU.max, ALU.subtract).then_inc(hT_lo, 1)

            def chain_first(j, layer, c, m):
                dve.wait_ge(gcols_done, j + 1)
                if layer == 0:
                    dve.wait_ge(bias_added, j + 1)
                nc.vector.scalar_tensor_tensor(by_batch(tile(0, c, m)), psW[:, :, 0:F], wback[:, layer:layer + 1],
                                               by_batch(tile(0, c, m)), ALU.mult, ALU.add).then_inc(g0_done, 1)
                nc.vector.tensor_reduce(tmax[:, c, bass.ds(m, 1)], last_of_chain(layer, c, m), AX.X, ALU.max,
                                        apply_absolute_value=True).then_inc(col_max, 1)

            def evacuate(q, m, bank, g):
                p, c = q // 2, q % 2
                t = tile(TARGET[p], c, m)
                dve.wait_ge(mm_done, g + 1)
                nc.vector.scalar_tensor_tensor(t, psA[:, bank, :], alpha[:, c, bass.ds(m, 1)], t,
                                               ALU.mult, ALU.add).then_inc(bank_free, 1)
                if p in (0, 2, 3):
                    dve.wait_ge(bank_free, g + 3)
                    nc.vector.tensor_reduce(tmax[:, c, bass.ds(m, 1)], t, AX.X, ALU.max,
                                            apply_absolute_value=True).then_inc(col_max, 1)

            MAXIMA = [M, 5 * M // 2, 3 * M, 4 * M, 5 * M, 6 * M + 1, 7 * M, 8 * M, 9 * M, 10 * M]

            def split_lo(q):
                c, layer = q % 2, LAYER[q // 2]
                dve.wait_ge(col_max, MAXIMA[q])
                nc.vector.tensor_tensor(dmax[:, c, :], tmax[:, c, :], dvec[:, layer, :], ALU.mult).then_inc(hm_step, 1)
                dve.wait_ge(hm_step, 2 * q + 1)
                nc.vector.tensor_reduce(hmax[:, c:c + 1], dmax[:, c, :], AX.X, ALU.max,
                                        apply_absolute_value=True).then_inc(half_max, 1)
                dve.wait_ge(half_gmax, q + 1)
                pq, rp = power_of_two(hgmax[:, c:c + 1], 4 + q, M + 1 + q + (q > 1))
                nc.vector.tensor_scalar(zback[:, c:c + 1], pq, 1.0 / PART, None, ALU.mult).then_inc(hm_step, 1)
                nc.vector.tensor_scalar(zscale[:, c, :], dvec[:, layer, :], rp, PART, ALU.mult,
                                        ALU.mult).then_inc(scale_ready, 1)
                dve.wait_ge(hm_step, 2 * q + 2)
                nc.vector.tensor_scalar(alpha[:, c, :], aback[:, layer, :], zback[:, c:c + 1], None, ALU.mult)
                dve.wait_ge(scale_ready, q + 1)
                with dve.Fori(0, M) as m:
                    dve.wait_ge(z_hi, m + M * q + 1)
                    nc.vector.scalar_tensor_tensor(Zl[:, c, m, :], SOURCE[q // 2](c, m), zscale[:, c, bass.ds(m, 1)],
                                                   Zh[:, c, m, :], ALU.mult, ALU.subtract).then_inc(z_lo, 1)

            nc.vector.memset(dvec[:, 1, :], 1.0).then_inc(bank_free, 2)
            nc.vector.memset(tmax[:, :, :], 0.0).then_inc(at_done, 2)
            nc.vector.memset(hmax[:, :], 0.0).then_inc(hT_lo, 1)
            nc.vector.memset(hgmax[:, :], 0.0).then_inc(g0_done, 1)
            for u in range(2):
                nc.vector.memset(pw[:, u, :], 0.0).then_inc(x_in[u], 16)

            dve.wait_ge(w_in0, 16)
            nc.vector.tensor_tensor(w0_in[:, 0, :], w0_in[:, 0, :], w0_in[:, 2, :], ALU.subtract).then_inc(w_combined, 1)
            nc.vector.tensor_scalar(w0_in[:, 2, :], w0_in[:, 2, :], 2.0, None, ALU.mult).then_inc(w_combined, 1)
            weights(0)

            with dve.Fori(0, PAIRS) as i:
                for u in range(2):
                    m = 2 * i + u
                    dve.wait_ge(x_in[u], 16 * i + 32)
                    normalise(m, u, 0, m)
                    dve.wait_ge(adj_in[u], 16 * i + 16)
                    nc.vector.tensor_reduce(amax[u][:, :], stage[u], AX.X, ALU.max,
                                            apply_absolute_value=True).then_inc(a_max, 1)
                    dve.wait_ge(a_max, m + 1)
                    p, rp = power_of_two(amax[u][:, :], 2 + u, m + 1)
                    nc.vector.tensor_scalar(aback[:, 1, bass.ds(m, 1)], p, 1.0 / PART, None, ALU.mult)
                    nc.vector.tensor_scalar(ascale[u][:, :], rp, PART, None, ALU.mult).then_inc(a_scale, 1)
                    chain_lo(m, u)
                    dve.wait_ge(at_hi, m + 1)
                    nc.vector.tensor_tensor(ATl[:, :, bass.ts(m, P)], psA[:, :, :].rearrange("p a (k m) -> p (a k) m", m=P),
                                            ATh[:, :, bass.ts(m, P)], ALU.subtract)
                    nc.vector.tensor_tensor(ADl[:, m, :], psT[:, 1, 0:P], ADh[:, m, :], ALU.subtract).then_inc(at_done, 1)
                    chain_first(m, 0, 0, m)

            dve.wait_ge(a_sum, M)
            nc.vector.tensor_tensor(dt[0][:, :], rowsum[:, :], aback[:, 1, :], ALU.mult).then_inc(dinv_step, 1)
            dve.wait_ge(dinv_step, 1)
            nc.vector.tensor_scalar(dt[1][:, :], dt[0][:, :], 0.0, None, ALU.is_gt).then_inc(dinv_step, 1)
            dve.wait_ge(dinv_step, 2)
            nc.vector.tensor_scalar(dt[4][:, :], dt[1][:, :], -1.0, 1.0, ALU.mult, ALU.add).then_inc(deg_parts, 1)
            nc.vector.tensor_tensor(dt[5][:, :], dt[0][:, :], dt[1][:, :], ALU.mult).then_inc(deg_parts, 1)
            dve.wait_ge(deg_parts, 2)
            nc.vector.tensor_tensor(dt[2][:, :], dt[5][:, :], dt[4][:, :], ALU.add).then_inc(dinv_step, 1)
            dve.wait_ge(dinv_step, 4)
            nc.vector.reciprocal(dt[6][:, :], dt[3][:, :]).then_inc(dinv_step, 1)
            dve.wait_ge(dinv_step, 5)
            nc.vector.tensor_tensor(dt[7][:, :], dt[6][:, :], dt[2][:, :], ALU.mult).then_inc(dinv_step, 1)
            dve.wait_ge(dinv_step, 6)
            nc.vector.tensor_tensor(dt[7][:, :], dt[7][:, :], dt[6][:, :], ALU.mult).then_inc(dinv_step, 1)
            dve.wait_ge(dinv_step, 7)
            nc.vector.tensor_scalar(dt[7][:, :], dt[7][:, :], -0.5, 1.5, ALU.mult, ALU.add).then_inc(dinv_step, 1)
            dve.wait_ge(dinv_step, 8)
            nc.vector.tensor_tensor(dt[7][:, :], dt[7][:, :], dt[6][:, :], ALU.mult).then_inc(dinv_step, 1)
            dve.wait_ge(dinv_step, 9)
            nc.vector.tensor_tensor(dvec[:, 0, :], dt[7][:, :], dt[1][:, :], ALU.mult).then_inc(dinv_step, 1)
            dve.wait_ge(dinv_step, 10)
            nc.vector.tensor_tensor(dt[0][:, :], dvec[:, 0, :], aback[:, 1, :], ALU.mult).then_inc(dinv_step, 1)
            dve.wait_ge(dinv_step, 11)
            nc.vector.tensor_scalar(aback[:, 0, :], dt[0][:, :], -1.0, None, ALU.mult).then_inc(dinv_step, 1)
            dve.wait_ge(dinv_step, 12)

            split_lo(0)
            with dve.Fori(0, PAIRS // 2) as i:
                for u in range(2):
                    m = 2 * i + u
                    for v in range(2):
                        j = 2 * m + v + M
                        dve.wait_ge(x_in[v], 16 * m + 16 * PAIRS + 32)
                        normalise(j, v, 1, 2 * m + v)
                        chain_lo(j, v)
                        chain_first(j, 0, 1, 2 * m + v)
                    evacuate(0, m, u, m)
            split_lo(1)
            dve.wait_ge(w_in1, 16)
            nc.vector.tensor_copy(wcat[1][:, 0, :], w1_in[:, :, 0]).then_inc(w_combined, 1)
            nc.vector.tensor_tensor(wcat[1][:, 1:4, :], w1_in[:, :, 1:4].rearrange("p o k -> p k o"),
                                    w1_in[:, :, 4:7].rearrange("p o k -> p k o"), ALU.add).then_inc(w_combined, 1)
            weights(1)
            with dve.Fori(0, PAIRS // 2) as i:
                for u in range(2):
                    m = 2 * i + u + M // 2
                    evacuate(0, m, u, m)
            split_lo(2)
            with dve.Fori(0, PAIRS) as i:
                for u in range(2):
                    evacuate(1, 2 * i + u, u, 2 * i + u + M)
            split_lo(3)

            def follow(c, m, u, g, j):
                chain_lo(j, 1 - u)
                evacuate(2 + c, m, u, g)
                dve.wait_ge(bank_free, g + 3)
                normalise(j + 1, u, c, m)
                chain_first(j, 1, c, m - 1)

            for c in range(2):
                g0 = (2 + c) * M
                if c == 0:
                    evacuate(2, 0, 0, g0)
                    dve.wait_ge(bank_free, g0 + 3)
                    normalise(J1, 0, 0, 0)
                else:
                    chain_lo(J1 + M - 1, 1)
                    evacuate(3, 0, 0, g0)
                    dve.wait_ge(bank_free, g0 + 3)
                    normalise(J1 + M, 0, 1, 0)
                    chain_first(J1 + M - 1, 1, 0, M - 1)
                    split_lo(4)
                with dve.Fori(0, PAIRS - 1) as i:
                    for u in (1, 0):
                        m = 2 * i + (1 if u else 2)
                        follow(c, m, u, m + g0, m - 1 + J1 + c * M)
                follow(c, M - 1, 1, g0 + M - 1, M - 2 + J1 + c * M)
            nc.vector.tensor_copy(ATl_diag, ADl[:, :, :]).then_inc(diag_lo, 1)
            chain_lo(J1 + 2 * M - 1, 1)
            evacuate(4, 0, 0, 4 * M)
            chain_first(J1 + 2 * M - 1, 1, 1, M - 1)
            split_lo(5)
            with dve.Fori(0, PAIRS - 1) as i:
                for u in (1, 0):
                    m = 2 * i + (1 if u else 2)
                    evacuate(4, m, u, m + 4 * M)
            evacuate(4, M - 1, 1, 5 * M - 1)
            split_lo(6)
            for q in range(5, 10):
                with dve.Fori(0, PAIRS) as i:
                    for u in range(2):
                        evacuate(q, 2 * i + u, u, 2 * i + u + q * M)
                if q + 2 < 10:
                    split_lo(q + 2)


_INS = ["x", "adj", "L0_gnn_Ws", "L0_gnn_bias", "L1_gnn_weight_1"]


def kernel(**inputs):
    import numpy as _np
    import concourse.bacc as _bacc
    from concourse import mybir as _mybir
    from concourse.bass_utils import run_bass_kernel_spmd as _run

    nc = _bacc.Bacc("TRN2", target_bir_lowering=False, num_devices=1)
    arrays, args = {}, []
    for name in _INS:
        a = _np.ascontiguousarray(inputs[name])
        arrays[f"in_{name}_dram"] = a
        args.append(nc.dram_tensor(f"in_{name}_dram", a.shape, _mybir.dt.from_np(a.dtype), kind="ExternalInput").ap())
    shape = arrays["in_x_dram"].shape
    args.append(nc.dram_tensor("out_0_dram", shape, _mybir.dt.float32, kind="ExternalOutput").ap())
    build(nc, *args)
    r = _run(nc, [arrays], core_ids=[0])
    return r.results[0]["out_0_dram"]
```

```python
from contextlib import ExitStack

import concourse.bass as bass
from concourse import mybir

F32 = mybir.dt.float32
F16 = mybir.dt.float16
BF16 = mybir.dt.bfloat16
I32 = mybir.dt.int32
ALU = mybir.AluOpType
ACT = mybir.ActivationFunctionType
AX = mybir.AxisListType
ABSMAX = bass.bass_isa.ReduceOp.absmax

P = 128
EXPONENT = 0x7F800000
TINY = 2.0 ** -100
PART = 2.0 ** 14
H_SCALE = 2.0 ** 11
EPS = 1e-5


def build(nc, x, adj_t, w0, bias, w1, out):
    T2, _, HC = x.shape
    M = T2 // 2
    N = M * P
    F = bias.shape[0]
    HB = HC // F
    NB = [3, 4]
    DIAG = N + P
    J1 = 2 * M
    LOADS = M // 2
    BOUND = PART / (F * 2)

    adj_pairs = adj_t.rearrange("(i k p) m -> i p k m", p=P, k=2)
    x_pairs = x.rearrange("(i k) p n -> i p k n", k=2)

    with ExitStack() as ctx:
        def sb(name, shape, dt=F32):
            return ctx.enter_context(nc.sbuf_tensor(name, shape, dt))

        def sem(name):
            return ctx.enter_context(nc.semaphore(name))

        G = sb("G", [P, 3, 2 * M, HC])
        work = sb("work", [P, 4 * N])
        stage = [work[:, h * 2 * N:(h + 1) * 2 * N].rearrange("p (k m) -> p k m", k=2) for h in range(2)]
        Zt = sb("Zt", [P, 2, 2, M, HC], F16)
        Z2 = work[:, :].bitcast(F16).rearrange("p (e m n) -> p e m n", e=2, m=M)
        Zh = [Zt[:, 0, 0], Zt[:, 1, 0], Z2[:, 0]]
        Zl = [Zt[:, 0, 1], Zt[:, 1, 1], Z2[:, 1]]
        ATh_all = sb("ATh", [P, M * DIAG], F16)
        ATl_all = sb("ATl", [P, M * DIAG], F16)
        ATh, ATl = (t[:, 0:M * N].rearrange("p (k m) -> p k m", k=M) for t in (ATh_all, ATl_all))
        ATh_diag, ATl_diag = (t[:, :].rearrange("p (k m) -> p k m", m=DIAG)[:, :, 0:P]
                              for t in (ATh_all, ATl_all))
        ADh = sb("ADh", [P, M, P], F16)
        ADl = sb("ADl", [P, M, P], F16)
        xn = [sb(f"xn{u}", [P, HC]) for u in range(2)]
        hTh = [sb(f"hTh{u}", [P, HC], F16) for u in range(2)]
        hTl = [sb(f"hTl{u}", [P, HC], F16) for u in range(2)]
        w0_in = sb("w0_in", [P, 3, F])
        w1_in = sb("w1_in", [P, 7, F])
        wcat = [w0_in, w1_in]
        Wh = [sb(f"Wh{i}", [P, NB[i] * F], F16) for i in range(2)]
        Wl = [sb(f"Wl{i}", [P, NB[i] * F], F16) for i in range(2)]
        ident = sb("ident", [P, P])
        offdiag = sb("offdiag", [P, P], F16)
        bias_b = sb("bias_b", [P, F])
        junk = [Zh[1][:, 2 * v:2 * v + N // HC, :].rearrange("p m n -> p (m n)") for v in range(2)]

        bn6 = sb("bn6", [P, 2, HB, 6])
        moments = sb("moments", [P, 2, HB, 2])
        var, sd, r0, nt, nt2, rstd, shift = (sb(n, [P, 2, HB]) for n in "var sd r0 nt nt2 rstd shift".split())
        wmax = sb("wmax", [P, 2])
        wgmax = sb("wgmax", [P, 2])
        wscale = sb("wscale", [P, 2])
        wback = sb("wback", [P, 2])
        asum = [sb(f"asum{h}", [P, 2]) for h in range(2)]
        ascale = [sb(f"ascale{h}", [P, 2]) for h in range(2)]
        aback = sb("aback", [P, M])
        abackb = [sb(f"abackb{h}", [P, 2], BF16) for h in range(2)]
        avec = sb("avec", [P, 2, M])
        dinv = sb("dinv", [P, M])
        frow = sb("frow", [P, 2, M])
        fmax = sb("fmax", [P, 2])
        fgmax = sb("fgmax", [P, 2])
        zw = sb("zw", [P, 2, M])
        zscale0 = sb("zscale0", [P, M])
        alpha0 = sb("alpha0", [P, 2, M])
        fb = sb("fb", [P, 4])
        dt = [sb(f"dt{i}", [P, M]) for i in range(8)]
        tmax = sb("tmax", [P, 2, M])
        dmax = sb("dmax", [P, 2, M])
        hmax = sb("hmax", [P, 2])
        hgmax = sb("hgmax", [P, 2])
        zscale = sb("zscale", [P, 2, M])
        zback = sb("zback", [P, 2])
        alpha = sb("alpha", [P, 2, M])
        pw = sb("pw", [P, 16, 6])

        psA = ctx.enter_context(nc.psum_tensor("psA", [P, 2, 512], F32))
        psT = ctx.enter_context(nc.psum_tensor("psT", [P, 2, 512], F32))
        psW = ctx.enter_context(nc.psum_tensor("psW", [P, HB, 512], F32))
        psD = psA[:, 0, 0:M * M]

        adj_in = [sem(f"adj_in{u}") for u in range(2)]
        x_in = [sem(f"x_in{u}") for u in range(2)]
        names = """w_in0 w_in1 bias_in out_done consts w_combined w_max w_gmax w_scale w_hi w_lo pow2_step
            a_sum a_scale at_hi at_lo ad_copied at_masked degrees deg_read deg_parts dinv_step f_step f_max f_gmax
            f_scaled ln_stats ln_moments ln_var ln_sd ln_r0 ln_n1 ln_n2 ln_n3 ln_rstd ln_n4 ln_shift xn_done xT_done
            hT_hi hT_lo hw_done cols_done psW_free bias_added row_max mm_done bank_free
            hm_step half_max half_gmax scale_ready z_hi z_lo zc_lo diag_hi diag_lo""".split()
        S = {n: sem(n) for n in names}
        (w_in0, w_in1, bias_in, out_done, consts, w_combined, w_max, w_gmax, w_scale, w_hi, w_lo, pow2_step,
         a_sum, a_scale, at_hi, at_lo, ad_copied, at_masked, degrees, deg_read, deg_parts, dinv_step, f_step, f_max,
         f_gmax, f_scaled, ln_stats, ln_moments, ln_var, ln_sd, ln_r0, ln_n1, ln_n2, ln_n3, ln_rstd, ln_n4, ln_shift,
         xn_done, xT_done, hT_hi, hT_lo, hw_done, cols_done, psW_free, bias_added, row_max, mm_done,
         bank_free, hm_step, half_max, half_gmax, scale_ready, z_hi, z_lo, zc_lo, diag_hi,
         diag_lo) = (S[n] for n in names)

        def tile(j, t):
            return G[:, j, t, :]

        def by_batch(ap):
            return ap.rearrange("p (b f) -> p b f", f=F)

        TARGET = [1, 0, 2, 1, 0]
        SOURCE = {0: 2, 2: 1, 3: 1, 6: 2, 7: 2, 8: 1, 9: 1}
        SPLIT_NO = {0: 0, 2: 1, 3: 2, 6: 3, 7: 4, 8: 5, 9: 6}

        block = ctx.enter_context(nc.Block())

        @block.sync
        def _(sp):
            sp.dma_start(w0_in[:, :, :], w0.rearrange("k i o -> i k o")).then_inc(w_in0, 16)
            for i in range(2 * LOADS):
                if i >= 2:
                    sp.wait_ge(x_in[i % 2], 16 * (i // 2))
                sp.dma_start(G[:, 0, 2 * i:2 * i + 2, :], x_pairs[i]).then_inc(x_in[i % 2], 16)
                if i < LOADS:
                    if i >= 2:
                        sp.wait_ge(at_lo, i - 1)
                    sp.dma_start(stage[i % 2], adj_pairs[i]).then_inc(adj_in[i % 2], 16)
                if i == 0:
                    sp.dma_start(bias_b[:, :], bias.partition_broadcast(P)).then_inc(bias_in, 16)
            sp.dma_start(w1_in[:, :, :], w1.rearrange("k i o -> i k o")).then_inc(w_in1, 16)
            with sp.Fori(0, 2 * M) as t:
                sp.wait_ge(bank_free, t + 8 * M + 3)
                sp.dma_start(out[t], tile(0, t)).then_inc(out_done, 16)
            sp.wait_ge(out_done, 16 * 2 * M)

        @block.gpsimd
        def _(pool):
            nc.gpsimd.memset(ident[:, :], 0.0).then_inc(consts, 1)
            nc.gpsimd.memset(offdiag[:, :], 1.0).then_inc(consts, 1)
            pool.wait_ge(consts, 2)
            for t, v in ((ident, 1.0), (offdiag, 0.0)):
                nc.gpsimd.affine_select(out=t[:, :], in_=t[:, :], compare_op=ALU.not_equal, fill=v, base=0,
                                        pattern=[[-1, P]], channel_multiplier=1).then_inc(consts, 1)
            pool.wait_ge(w_max, 1)
            nc.gpsimd.partition_all_reduce(wgmax[:, 0:1], wmax[:, 0:1], P, ABSMAX).then_inc(w_gmax, 1)
            pool.wait_ge(consts, 4)
            pool.wait_ge(bias_in, 16)

            def add_bias(t):
                pool.wait_ge(xn_done, t + 1)
                pool.nop(nofuse=True)
                nc.gpsimd.tensor_tensor(by_batch(tile(0, t)), by_batch(tile(0, t)),
                                        bias_b[:, :].unsqueeze(1).broadcast_to([P, HB, F]), ALU.add).then_inc(bias_added, 1)

            with pool.Fori(0, LOADS) as i:
                add_bias(2 * i)
                add_bias(2 * i + 1)
                pool.wait_ge(at_lo, i + 1)
                for v in range(2):
                    for at, ad in ((ATh_diag, ADh), (ATl_diag, ADl)):
                        nc.gpsimd.tensor_copy(ad[:, 2 * i + v, :], at[:, 2 * i + v, :]).then_inc(ad_copied, 1)
                pool.wait_ge(ad_copied, 4 * i + 4)
                pool.nop(nofuse=True)
                for v in range(2):
                    for at in (ATh_diag, ATl_diag):
                        last = nc.gpsimd.tensor_tensor(at[:, 2 * i + v, :], at[:, 2 * i + v, :], offdiag[:, :], ALU.mult)
                last.then_inc(at_masked, 1)

            for i in range(2):
                pool.wait_ge(f_max, i + 1)
                nc.gpsimd.partition_all_reduce(fgmax[:, i:i + 1], fmax[:, i:i + 1], P, ABSMAX).then_inc(f_gmax, 1)
            with pool.Fori(M, 2 * M) as t:
                add_bias(t)
            pool.wait_ge(w_max, 2)
            nc.gpsimd.partition_all_reduce(wgmax[:, 1:2], wmax[:, 1:2], P, ABSMAX).then_inc(w_gmax, 1)
            for n, q in enumerate(q for q in SPLIT_NO if q):
                pool.wait_ge(half_max, n + 1)
                c = q % 2
                nc.gpsimd.partition_all_reduce(hgmax[:, c:c + 1], hmax[:, c:c + 1], P, ABSMAX).then_inc(half_gmax, 1)

        @block.scalar
        def _(act):
            def deviation(call, v):
                act.wait_ge(ln_var, call + 1)
                nc.scalar.activation(sd[:, v, :], var[:, v, :], ACT.Sqrt).then_inc(ln_sd, 1)

            def normalise(call, tiles):
                act.wait_ge(ln_shift, call + 1)
                for t, u in tiles:
                    for b in range(HB):
                        last = nc.scalar.activation(xn[u][:, b * F:(b + 1) * F], tile(0, t)[:, b * F:(b + 1) * F],
                                                    ACT.Identity, scale=rstd[:, u, b:b + 1], bias=shift[:, u, b:b + 1])
                    last.then_inc(xn_done, 1)

            def transposed_hi(j, u):
                act.wait_ge(xT_done, j + 1)
                nc.scalar.activation(hTh[u][:, :], psT[:, u, :], ACT.Relu).then_inc(hT_hi, 1)

            def columns(j, t, layer, z=None, m=None):
                act.wait_ge(hw_done, j + 1)
                last_block = NB[layer] - 1
                if z is not None:
                    nc.scalar.activation(by_batch(Zh[z][:, m, :]), psW[:, :, last_block * F:(last_block + 1) * F],
                                         ACT.Copy, scale=zw[:, layer, bass.ds(m, 1)])
                    last_block -= 1
                for k in range(1, last_block + 1):
                    last = nc.scalar.activation(by_batch(tile(k, t)), psW[:, :, k * F:(k + 1) * F], ACT.Copy,
                                                scale=wback[:, layer:layer + 1])
                last.then_inc(cols_done, 1)

            def weights_hi(layer):
                act.wait_ge(w_scale, layer + 1)
                nc.scalar.activation(Wh[layer][:, :], wcat[layer][:, 0:NB[layer], :].rearrange("p k o -> p (k o)"),
                                     ACT.Copy, scale=wscale[:, layer:layer + 1]).then_inc(w_hi, 1)

            def split_hi(q):
                c = q % 2
                act.wait_ge(scale_ready, SPLIT_NO[q] + 1)
                scale = zscale0[:, :] if q == 0 else zscale[:, c, :]
                with act.Fori(0, M) as m:
                    nc.scalar.activation(Zh[q % 3][:, m, :], tile(SOURCE[q], m + c * M), ACT.Copy,
                                         scale=scale[:, bass.ds(m, 1)]).then_inc(z_hi, 1)

            weights_hi(0)
            deviation(0, slice(0, 2))
            with act.Fori(0, LOADS // 2) as i:
                for h in range(2):
                    r = 2 * i + h
                    act.wait_ge(adj_in[h], 16 * i + 16)
                    for v in range(2):
                        last = nc.scalar.activation(junk[v], stage[h][:, v, :], ACT.Abs, accum_out=asum[h][:, v:v + 1])
                    last.then_inc(a_sum, 1)
                    normalise(r, [(2 * r, 0), (2 * r + 1, 1)])
                    act.wait_ge(a_scale, r + 1)
                    for v in range(2):
                        last = nc.scalar.activation(ATh[:, 2 * r + v, :], stage[h][:, v, :], ACT.Copy,
                                                    scale=ascale[h][:, v:v + 1])
                    last.then_inc(at_hi, 1)
                    for v in range(2):
                        transposed_hi(2 * r + v, v)
                    deviation(r + 1, slice(0, 2))
                    for v in range(2):
                        columns(2 * r + v, 2 * r + v, 0)
            normalise(LOADS, [(M, 0), (M + 1, 1)])
            act.wait_ge(dinv_step, 2)
            nc.scalar.activation(dt[3][:, :], dt[2][:, :], ACT.Sqrt).then_inc(dinv_step, 1)
            for v in range(2):
                transposed_hi(M + v, v)
            split_hi(0)
            act.wait_ge(f_scaled, 1)
            for s in range(LOADS):
                j = M + 2 * s
                if s:
                    for v in range(2):
                        transposed_hi(j + v, v)
                if s < LOADS - 1:
                    deviation(LOADS + s + 1, slice(0, 2))
                columns(j, j, 0, 1, j - M)
                if s < LOADS - 1:
                    normalise(LOADS + s + 1, [(j + 2, 0), (j + 3, 1)])
                columns(j + 1, j + 1, 0, 1, j + 1 - M)
            weights_hi(1)
            split_hi(2)

            def follow(c, m, u):
                j = m - 1 + J1 + c * M
                transposed_hi(j, 1 - u)
                deviation(j + 1 - J1 + 2 * LOADS, u)
                columns(j, m - 1 + c * M, 1, (4 + c) % 3, m - 1)
                normalise(j + 1 - J1 + 2 * LOADS, [(m + c * M, u)])

            for c in range(2):
                if c == 0:
                    deviation(2 * LOADS, 0)
                    normalise(2 * LOADS, [(0, 0)])
                    split_hi(3)
                    act.wait_ge(f_scaled, 3)
                else:
                    transposed_hi(J1 + M - 1, 1)
                    deviation(2 * LOADS + M, 0)
                    columns(J1 + M - 1, M - 1, 1, 1, M - 1)
                    normalise(2 * LOADS + M, [(M, 0)])
                with act.Fori(0, LOADS - 1) as i:
                    follow(c, 2 * i + 1, 1)
                    follow(c, 2 * i + 2, 0)
                follow(c, M - 1, 1)
            act.wait_ge(mm_done, 4 * M)
            nc.scalar.copy(ATh_diag, ADh[:, :, :]).then_inc(diag_hi, 1)
            transposed_hi(J1 + 2 * M - 1, 1)
            columns(J1 + 2 * M - 1, 2 * M - 1, 1, 2, M - 1)
            for q in (6, 7, 8, 9):
                split_hi(q)

        @block.tensor
        def _(pe):
            def products(q, m, bank, ks, arriving=False):
                zh, zl = Zh[q % 3], Zl[q % 3]
                for k in ks:
                    if arriving:
                        pe.wait_ge(z_lo, k + 1)
                    for a, z in ((ATh, zh), (ATh, zl), (ATl, zh)):
                        last = nc.tensor.matmul(psA[:, bank, :], a[:, k, bass.ts(m, P)], z[:, k, :],
                                                start=(k == 0 and z is zh and a is ATh),
                                                stop=(k == M - 1 and a is ATl))
                if ks[-1] == M - 1:
                    last.then_inc(mm_done, 1)

            def chain_transpose(j, u):
                pe.wait_ge(xn_done, j + 1)
                pe.wait_ge(hT_lo, j + 1)
                for b in range(HB):
                    last = nc.tensor.transpose(psT[:, u, b * F:(b + 1) * F], xn[u][:, b * F:(b + 1) * F], ident[:, :])
                last.then_inc(xT_done, 1)

            def chain_weights(j, u, layer):
                pe.wait_ge(hT_lo, j + 3)
                pe.wait_ge(psW_free, j + 1)
                n = NB[layer] * F
                for b in range(HB):
                    for h, w in ((hTh, Wh), (hTh, Wl), (hTl, Wh)):
                        last = nc.tensor.matmul(psW[:, b, 0:n], h[u][:, b * F:(b + 1) * F], w[layer][:, :],
                                                start=(h is hTh and w is Wh), stop=(h is hTl))
                last.then_inc(hw_done, 1)

            def slot(q, m, bank):
                pe.wait_ge(bank_free, m + q * M + 1)
                products(q, m, bank, range(M))

            def slot_with_chain(q, m, bank, j, u):
                pe.wait_ge(bank_free, m + q * M + 1)
                products(q, m, bank, range(M - 2))
                chain_transpose(j, u)
                products(q, m, bank, range(M - 2, M))
                chain_weights(j, u, 1)

            pe.wait_ge(consts, 4)
            pe.wait_ge(w_lo, 1)
            with pe.Fori(0, LOADS // 2) as i:
                for h in range(2):
                    r = 2 * i + h
                    for v in range(2):
                        chain_transpose(2 * r + v, v)
                    for v in range(2):
                        chain_weights(2 * r + v, v, 0)
                    pe.wait_ge(at_masked, r + 1)
                    for v in range(2):
                        for m in range(M):
                            for a in (ATh, ATl):
                                last = nc.tensor.matmul(psD[:, bass.ds((2 * r + v) * M + m, 1)],
                                                        a[:, 2 * r + v, m * P:(m + 1) * P], abackb[h][:, v:v + 1],
                                                        start=(a is ATh), stop=(a is ATl))
                    last.then_inc(degrees, 1)
            for s in range(LOADS):
                j = M + 2 * s
                for v in range(2):
                    chain_transpose(j + v, v)
                chain_weights(j, 0, 0)
                if s == 0:
                    pe.wait_ge(deg_read, 1)
                pe.wait_ge(bank_free, s + 1)
                products(0, s, s % 2, range(M - 3), arriving=(s == 0))
                chain_weights(j + 1, 1, 0)
                products(0, s, s % 2, range(M - 3, M), arriving=(s == 0))
            with pe.Fori(0, LOADS // 2) as i:
                for u in range(2):
                    slot(0, 2 * i + u + M // 2, u)
            pe.wait_ge(zc_lo, M)
            with pe.Fori(0, LOADS) as i:
                for u in range(2):
                    slot(1, 2 * i + u, u)
            pe.wait_ge(w_lo, 2)
            for c in range(2):
                q = 2 + c
                pe.wait_ge(z_lo, M * (SPLIT_NO[q] + 1))
                if c == 0:
                    slot(q, 0, 0)
                else:
                    slot_with_chain(q, 0, 0, J1 + M - 1, 1)
                with pe.Fori(0, LOADS - 1) as i:
                    for u in (1, 0):
                        m = 2 * i + (1 if u else 2)
                        slot_with_chain(q, m, u, m - 1 + J1 + c * M, 1 - u)
                slot_with_chain(q, M - 1, 1, M - 2 + J1 + c * M, 0)
            pe.wait_ge(diag_hi, 1)
            pe.wait_ge(diag_lo, 1)
            pe.wait_ge(zc_lo, 2 * M)
            slot_with_chain(4, 0, 0, J1 + 2 * M - 1, 1)
            with pe.Fori(0, LOADS - 1) as i:
                for u in (1, 0):
                    slot(4, 2 * i + (1 if u else 2), u)
            slot(4, M - 1, 1)
            for q in range(5, 10):
                if q == 5:
                    pe.wait_ge(zc_lo, 3 * M)
                else:
                    pe.wait_ge(z_lo, M * (SPLIT_NO[q] + 1))
                with pe.Fori(0, LOADS) as i:
                    for u in range(2):
                        slot(q, 2 * i + u, u)

        @block.vector
        def _(dve):
            def powers(src, n, w, call):
                t = pw[:, n, :]
                nc.vector.tensor_scalar(t[:, 0:w], src, TINY, None, ALU.max).then_inc(pow2_step, 1)
                dve.wait_ge(pow2_step, 3 * call + 1)
                nc.vector.tensor_scalar(t[:, 2:2 + w].bitcast(I32), t[:, 0:w].bitcast(I32), EXPONENT, None,
                                        ALU.bitwise_and).then_inc(pow2_step, 1)
                dve.wait_ge(pow2_step, 3 * call + 2)
                nc.vector.reciprocal(t[:, 4:4 + w], t[:, 2:2 + w]).then_inc(pow2_step, 1)
                dve.wait_ge(pow2_step, 3 * call + 3)
                return t[:, 2:2 + w], t[:, 4:4 + w]

            CALL = {"w0": 0, "f0": 1 + LOADS, "w1": 2 + LOADS, 2: 3 + LOADS, "f1": 4 + LOADS,
                    3: 5 + LOADS, 6: 6 + LOADS, 7: 7 + LOADS, 8: 8 + LOADS, 9: 9 + LOADS}
            SLOT_OF_PW = {k: n for n, k in enumerate(["a0", "a1", *CALL])}

            def weights(layer):
                cat = wcat[layer][:, 0:NB[layer], :].rearrange("p k o -> p (k o)")
                dve.wait_ge(w_combined, 2 * layer + 1)
                if layer == 0:
                    dve.wait_ge(w_combined, 2)
                nc.vector.tensor_reduce(wmax[:, layer:layer + 1], cat, AX.X, ALU.max,
                                        apply_absolute_value=True).then_inc(w_max, 1)
                dve.wait_ge(w_gmax, layer + 1)
                p, rp = powers(wgmax[:, layer:layer + 1], SLOT_OF_PW[f"w{layer}"], 1, CALL[f"w{layer}"])
                nc.vector.tensor_scalar(wback[:, layer:layer + 1], p, 1.0 / (PART * H_SCALE), None, ALU.mult)
                nc.vector.tensor_scalar(wscale[:, layer:layer + 1], rp, PART, None, ALU.mult).then_inc(w_scale, 1)
                dve.wait_ge(w_scale, layer + 1)
                dve.wait_ge(w_hi, layer + 1)
                nc.vector.scalar_tensor_tensor(Wl[layer][:, :], cat, wscale[:, layer:layer + 1], Wh[layer][:, :],
                                               ALU.mult, ALU.subtract).then_inc(w_lo, 1)

            def statistics(call, tiles, v):
                dve.nop(nofuse=True)
                for t, u in tiles:
                    for b in range(HB):
                        last = nc.vector.bn_stats(bn6[:, u, b, :], tile(0, t)[:, b * F:(b + 1) * F])
                last.then_inc(ln_stats, 1)
                dve.wait_ge(ln_stats, call + 1)
                dve.nop(nofuse=True)
                for t, u in tiles:
                    for b in range(HB):
                        last = nc.vector.bn_aggr(moments[:, u, b, :], bn6[:, u, b, :])
                last.then_inc(ln_moments, 1)
                dve.wait_ge(ln_moments, call + 1)
                nc.vector.tensor_scalar(var[:, v, :], moments[:, v, :, 1], EPS, None, ALU.add).then_inc(ln_var, 1)

            def factors(call, v):
                dve.wait_ge(ln_sd, call + 1)
                nc.vector.reciprocal(r0[:, v, :], sd[:, v, :]).then_inc(ln_r0, 1)
                dve.wait_ge(ln_r0, call + 1)
                nc.vector.tensor_tensor(nt[:, v, :], r0[:, v, :], var[:, v, :], ALU.mult).then_inc(ln_n1, 1)
                dve.wait_ge(ln_n1, call + 1)
                nc.vector.tensor_tensor(nt2[:, v, :], nt[:, v, :], r0[:, v, :], ALU.mult).then_inc(ln_n2, 1)
                dve.wait_ge(ln_n2, call + 1)
                nc.vector.tensor_scalar(nt[:, v, :], nt2[:, v, :], -0.5 * H_SCALE, 1.5 * H_SCALE, ALU.mult,
                                        ALU.add).then_inc(ln_n3, 1)
                dve.wait_ge(ln_n3, call + 1)
                nc.vector.tensor_tensor(rstd[:, v, :], nt[:, v, :], r0[:, v, :], ALU.mult).then_inc(ln_rstd, 1)
                dve.wait_ge(ln_rstd, call + 1)
                nc.vector.tensor_tensor(nt2[:, v, :], moments[:, v, :, 0], rstd[:, v, :], ALU.mult).then_inc(ln_n4, 1)
                dve.wait_ge(ln_n4, call + 1)
                nc.vector.tensor_scalar(shift[:, v, :], nt2[:, v, :], -1.0, None, ALU.mult).then_inc(ln_shift, 1)

            def transposed_lo(j, u):
                dve.wait_ge(hT_hi, j + 1)
                nc.vector.scalar_tensor_tensor(hTl[u][:, :], psT[:, u, :], 0.0, hTh[u][:, :],
                                               ALU.max, ALU.subtract).then_inc(hT_lo, 1)

            def first_columns(j, t, layer, z=None, m=None):
                dve.wait_ge(cols_done, j + 1)
                if z is not None:
                    k = NB[layer] - 1
                    nc.vector.scalar_tensor_tensor(by_batch(Zl[z][:, m, :]), psW[:, :, k * F:(k + 1) * F],
                                                   zw[:, layer, bass.ds(m, 1)], by_batch(Zh[z][:, m, :]),
                                                   ALU.mult, ALU.subtract).then_inc(zc_lo, 1)
                if layer == 0:
                    dve.wait_ge(bias_added, j + 1)
                nc.vector.scalar_tensor_tensor(by_batch(tile(0, t)), psW[:, :, 0:F], wback[:, layer:layer + 1],
                                               by_batch(tile(0, t)), ALU.mult, ALU.add).then_inc(psW_free, 1)

            def evacuate(q, m, bank):
                p, c = q // 2, q % 2
                g = m + q * M
                t = tile(TARGET[p], m + c * M)
                back = alpha0[:, p // 2, :] if p in (0, 2) else alpha[:, c, :]
                dve.wait_ge(mm_done, g + 1)
                nc.vector.scalar_tensor_tensor(t, psA[:, bank, :], back[:, bass.ds(m, 1)], t,
                                               ALU.mult, ALU.add).then_inc(bank_free, 1)
                if p in (0, 2, 3):
                    dve.wait_ge(bank_free, g + 3)
                    nc.vector.tensor_reduce(tmax[:, c, bass.ds(m, 1)], t, AX.X, ALU.max,
                                            apply_absolute_value=True).then_inc(row_max, 1)

            def half_maximum(q):
                c, layer, n = q % 2, int(q >= 4), SPLIT_NO[q]
                dve.wait_ge(row_max, M * n)
                nc.vector.tensor_tensor(dmax[:, c, :], tmax[:, c, :], frow[:, layer, :], ALU.mult).then_inc(hm_step, 1)
                dve.wait_ge(hm_step, 2 * n - 1)
                nc.vector.tensor_reduce(hmax[:, c:c + 1], dmax[:, c, :], AX.X, ALU.max,
                                        apply_absolute_value=True).then_inc(half_max, 1)

            def half_scale(q):
                c, layer, n = q % 2, int(q >= 4), SPLIT_NO[q]
                dve.wait_ge(half_gmax, n)
                pq, rp = powers(hgmax[:, c:c + 1], SLOT_OF_PW[q], 1, CALL[q])
                nc.vector.tensor_scalar(zscale[:, c, :], frow[:, layer, :], rp, PART, ALU.mult,
                                        ALU.mult).then_inc(scale_ready, 1)
                nc.vector.tensor_scalar(zback[:, c:c + 1], pq, 1.0 / PART, None, ALU.mult).then_inc(hm_step, 1)
                dve.wait_ge(hm_step, 2 * n)
                nc.vector.tensor_scalar(alpha[:, c, :], avec[:, layer, :], zback[:, c:c + 1], None, ALU.mult)
                dve.wait_ge(scale_ready, n + 1)

            def split_lo(q, first, n):
                c = q % 2
                scale = zscale0[:, :] if q == 0 else zscale[:, c, :]
                with dve.Fori(first, first + n) as m:
                    dve.wait_ge(z_hi, m + M * SPLIT_NO[q] + 1)
                    nc.vector.scalar_tensor_tensor(Zl[q % 3][:, m, :], tile(SOURCE[q], m + c * M),
                                                   scale[:, bass.ds(m, 1)], Zh[q % 3][:, m, :],
                                                   ALU.mult, ALU.subtract).then_inc(z_lo, 1)

            def layer_scale(layer):
                dve.wait_ge(f_gmax, layer + 1)
                wp = pw[:, SLOT_OF_PW[f"w{layer}"], :]
                pf, rpf = powers(fgmax[:, layer:layer + 1], SLOT_OF_PW[f"f{layer}"], 1, CALL[f"f{layer}"])
                f = fb[:, 2 * layer:2 * layer + 1]
                b = fb[:, 2 * layer + 1:2 * layer + 2]
                nc.vector.tensor_scalar(f, rpf, wp[:, 4:5], BOUND, ALU.mult, ALU.mult).then_inc(f_step, 1)
                nc.vector.tensor_scalar(b, pf, wp[:, 2:3], 1.0 / BOUND, ALU.mult, ALU.mult).then_inc(f_step, 1)
                dve.wait_ge(f_step, 2 * layer + 2)
                if layer == 0:
                    nc.vector.tensor_scalar(zscale0[:, :], frow[:, 0, :], f, None, ALU.mult).then_inc(scale_ready, 1)
                nc.vector.tensor_scalar(zw[:, layer, :], frow[:, layer, :], f, wback[:, layer:layer + 1],
                                        ALU.mult, ALU.mult).then_inc(f_scaled, 1)
                nc.vector.tensor_scalar(alpha0[:, layer, :], avec[:, layer, :], b, None, ALU.mult).then_inc(f_scaled, 1)
                dve.wait_ge(f_scaled, 2 * layer + 2)

            nc.vector.memset(avec[:, 1, :], 1.0).then_inc(bank_free, 2)
            nc.vector.memset(tmax[:, :, :], 0.0).then_inc(hT_lo, 2)
            nc.vector.memset(pw[:, 0, :], 0.0).then_inc(psW_free, 1)

            dve.wait_ge(w_in0, 16)
            nc.vector.tensor_tensor(w0_in[:, 0, :], w0_in[:, 0, :], w0_in[:, 2, :], ALU.subtract).then_inc(w_combined, 1)
            nc.vector.tensor_scalar(w0_in[:, 2, :], w0_in[:, 2, :], 2.0, None, ALU.mult).then_inc(w_combined, 1)
            weights(0)

            dve.wait_ge(x_in[0], 16)
            statistics(0, [(0, 0), (1, 1)], slice(0, 2))
            with dve.Fori(0, LOADS // 2) as i:
                for h in range(2):
                    r = 2 * i + h
                    factors(r, slice(0, 2))
                    dve.wait_ge(a_sum, r + 1)
                    p, rp = powers(asum[h][:, :], h, 2, r + 1)
                    nc.vector.tensor_scalar(ascale[h][:, :], rp, PART, None, ALU.mult).then_inc(a_scale, 1)
                    nc.vector.tensor_scalar(aback[:, bass.ds(2 * r, 2)], p, 1.0 / PART, None, ALU.mult)
                    nc.vector.tensor_scalar(abackb[h][:, :], p, 1.0 / PART, None, ALU.mult)
                    dve.wait_ge(a_scale, r + 1)
                    dve.wait_ge(at_hi, r + 1)
                    for v in range(2):
                        last = nc.vector.scalar_tensor_tensor(ATl[:, 2 * r + v, :], stage[h][:, v, :],
                                                              ascale[h][:, v:v + 1], ATh[:, 2 * r + v, :],
                                                              ALU.mult, ALU.subtract)
                    last.then_inc(at_lo, 1)
                    for v in range(2):
                        transposed_lo(2 * r + v, v)
                    dve.wait_ge(x_in[1 - h], 16 * i + 16 * h + 16)
                    statistics(r + 1, [(2 * r + 2, 0), (2 * r + 3, 1)], slice(0, 2))
                    for v in range(2):
                        first_columns(2 * r + v, 2 * r + v, 0)
            factors(LOADS, slice(0, 2))

            dve.wait_ge(degrees, LOADS)
            nc.vector.tensor_reduce(dt[0][:, :], psD.rearrange("p (k m) -> p m k", m=M), AX.X, ALU.add).then_inc(deg_read, 1)
            dve.wait_ge(deg_read, 1)
            nc.vector.tensor_scalar(dt[1][:, :], dt[0][:, :], 0.0, None, ALU.is_gt).then_inc(dinv_step, 1)
            dve.wait_ge(dinv_step, 1)
            nc.vector.tensor_scalar(dt[4][:, :], dt[1][:, :], -1.0, 1.0, ALU.mult, ALU.add).then_inc(deg_parts, 1)
            nc.vector.tensor_tensor(dt[5][:, :], dt[0][:, :], dt[1][:, :], ALU.mult).then_inc(deg_parts, 1)
            dve.wait_ge(deg_parts, 2)
            nc.vector.tensor_tensor(dt[2][:, :], dt[5][:, :], dt[4][:, :], ALU.add).then_inc(dinv_step, 1)
            dve.wait_ge(dinv_step, 3)
            nc.vector.reciprocal(dt[6][:, :], dt[3][:, :]).then_inc(dinv_step, 1)
            dve.wait_ge(dinv_step, 4)
            nc.vector.tensor_tensor(dt[7][:, :], dt[6][:, :], dt[2][:, :], ALU.mult).then_inc(dinv_step, 1)
            dve.wait_ge(dinv_step, 5)
            nc.vector.tensor_tensor(dt[4][:, :], dt[7][:, :], dt[6][:, :], ALU.mult).then_inc(dinv_step, 1)
            dve.wait_ge(dinv_step, 6)
            nc.vector.tensor_scalar(dt[5][:, :], dt[4][:, :], -0.5, 1.5, ALU.mult, ALU.add).then_inc(dinv_step, 1)
            dve.wait_ge(dinv_step, 7)
            nc.vector.tensor_tensor(dt[7][:, :], dt[5][:, :], dt[6][:, :], ALU.mult).then_inc(dinv_step, 1)
            dve.wait_ge(dinv_step, 8)
            nc.vector.tensor_tensor(dinv[:, :], dt[7][:, :], dt[1][:, :], ALU.mult).then_inc(dinv_step, 1)
            dve.wait_ge(dinv_step, 9)
            nc.vector.tensor_tensor(frow[:, 0, :], dinv[:, :], aback[:, :], ALU.mult).then_inc(dinv_step, 1)
            nc.vector.tensor_scalar(avec[:, 0, :], dinv[:, :], -1.0, None, ALU.mult)
            nc.vector.tensor_copy(frow[:, 1, :], aback[:, :]).then_inc(dinv_step, 1)
            dve.wait_ge(dinv_step, 11)
            nc.vector.tensor_reduce(fmax[:, 0:1], frow[:, 0, :], AX.X, ALU.max).then_inc(f_max, 1)
            nc.vector.tensor_reduce(fmax[:, 1:2], frow[:, 1, :], AX.X, ALU.max).then_inc(f_max, 1)
            for v in range(2):
                transposed_lo(M + v, v)
            layer_scale(0)
            split_lo(0, 0, M)
            for s in range(LOADS):
                j = M + 2 * s
                if s:
                    for v in range(2):
                        transposed_lo(j + v, v)
                if s < LOADS - 1:
                    dve.wait_ge(x_in[(s + 1) % 2], 16 * (LOADS // 2 + (s + 1) // 2 + 1))
                    statistics(LOADS + s + 1, [(j + 2, 0), (j + 3, 1)], slice(0, 2))
                first_columns(j, j, 0, 1, j - M)
                if s < LOADS - 1:
                    factors(LOADS + s + 1, slice(0, 2))
                first_columns(j + 1, j + 1, 0, 1, j + 1 - M)
                evacuate(0, s, s % 2)
            dve.wait_ge(w_in1, 16)
            nc.vector.tensor_tensor(w1_in[:, 1:4, :], w1_in[:, 1:4, :], w1_in[:, 4:7, :], ALU.add).then_inc(w_combined, 1)
            weights(1)
            with dve.Fori(0, LOADS // 2) as i:
                for u in range(2):
                    evacuate(0, 2 * i + u + M // 2, u)
            half_maximum(2)
            evacuate(1, 0, 0)
            half_scale(2)
            split_lo(2, 0, M // 2)
            evacuate(1, 1, 1)
            split_lo(2, M // 2, M // 2)
            with dve.Fori(1, LOADS) as i:
                for u in range(2):
                    evacuate(1, 2 * i + u, u)
            layer_scale(1)
            half_maximum(3)

            def follow(c, m, u):
                j = m - 1 + J1 + c * M
                transposed_lo(j, 1 - u)
                evacuate(2 + c, m, u)
                dve.wait_ge(bank_free, m + (2 + c) * M + 3)
                statistics(j + 1 - J1 + 2 * LOADS, [(m + c * M, u)], u)
                factors(j + 1 - J1 + 2 * LOADS, u)
                first_columns(j, m - 1 + c * M, 1, (4 + c) % 3, m - 1)

            for c in range(2):
                g0 = (2 + c) * M
                if c == 0:
                    evacuate(2, 0, 0)
                    dve.wait_ge(bank_free, g0 + 3)
                    statistics(2 * LOADS, [(0, 0)], 0)
                    factors(2 * LOADS, 0)
                    half_scale(3)
                    split_lo(3, 0, M)
                else:
                    transposed_lo(J1 + M - 1, 1)
                    evacuate(3, 0, 0)
                    dve.wait_ge(bank_free, g0 + 3)
                    statistics(2 * LOADS + M, [(M, 0)], 0)
                    factors(2 * LOADS + M, 0)
                    first_columns(J1 + M - 1, M - 1, 1, 1, M - 1)
                with dve.Fori(0, LOADS - 1) as i:
                    follow(c, 2 * i + 1, 1)
                    follow(c, 2 * i + 2, 0)
                follow(c, M - 1, 1)
            nc.vector.tensor_copy(ATl_diag, ADl[:, :, :]).then_inc(diag_lo, 1)
            transposed_lo(J1 + 2 * M - 1, 1)
            evacuate(4, 0, 0)
            first_columns(J1 + 2 * M - 1, 2 * M - 1, 1, 2, M - 1)
            with dve.Fori(0, LOADS - 1) as i:
                evacuate(4, 2 * i + 1, 1)
                evacuate(4, 2 * i + 2, 0)
            evacuate(4, M - 1, 1)
            for q in range(5, 10):
                if q < 9:
                    half_maximum(q + 1)
                evacuate(q, 0, 0)
                if q < 9:
                    half_scale(q + 1)
                    split_lo(q + 1, 0, M // 2)
                evacuate(q, 1, 1)
                if q < 9:
                    split_lo(q + 1, M // 2, M // 2)
                with dve.Fori(1, LOADS) as i:
                    for u in range(2):
                        evacuate(q, 2 * i + u, u)


_INS = ["x", "adj", "L0_gnn_Ws", "L0_gnn_bias", "L1_gnn_weight_1"]


def kernel(**inputs):
    import numpy as _np
    import concourse.bacc as _bacc
    from concourse import mybir as _mybir
    from concourse.bass_utils import run_bass_kernel_spmd as _run

    nc = _bacc.Bacc("TRN2", target_bir_lowering=False, num_devices=1)
    a = {n: _np.asarray(inputs[n]) for n in _INS}
    B, N, F = a["x"].shape
    a["x"] = a["x"].reshape(2, B // 2, N // P, P, F).transpose(0, 2, 3, 1, 4).reshape(2 * N // P, P, B // 2 * F)
    a["adj"] = a["adj"].T
    a["L1_gnn_weight_1"] = a["L1_gnn_weight_1"].transpose(2, 0, 1)
    arrays, args = {}, []
    for name in _INS:
        v = _np.ascontiguousarray(a[name])
        arrays[f"in_{name}_dram"] = v
        args.append(nc.dram_tensor(f"in_{name}_dram", v.shape, _mybir.dt.from_np(v.dtype), kind="ExternalInput").ap())
    shape = arrays["in_x_dram"].shape
    args.append(nc.dram_tensor("out_0_dram", shape, _mybir.dt.float32, kind="ExternalOutput").ap())
    build(nc, *args)
    r = _run(nc, [arrays], core_ids=[0])
    y = r.results[0]["out_0_dram"].reshape(2, N // P, P, B // 2, F)
    return _np.ascontiguousarray(y.transpose(0, 3, 1, 2, 4).reshape(B, N, F))
```

```python
from contextlib import ExitStack

import concourse.bass as bass
from concourse import mybir

F32 = mybir.dt.float32
F16 = mybir.dt.float16
BF16 = mybir.dt.bfloat16
I32 = mybir.dt.int32
ALU = mybir.AluOpType
ACT = mybir.ActivationFunctionType
AX = mybir.AxisListType
ABSMAX = bass.bass_isa.ReduceOp.absmax

P = 128
EXPONENT = 0x7F800000
TINY = 2.0 ** -100
PART = 2.0 ** 14
H_SCALE = 2.0 ** 11
EPS = 1e-5


def build(nc, x, adj_t, w0, bias, w1, out):
    T2, _, HC = x.shape
    M = T2 // 2
    N = M * P
    F = bias.shape[0]
    HB = HC // F
    NB = [3, 4]
    DIAG = N + P
    J1 = 2 * M
    LOADS = M // 2
    EARLY = 2
    BOUND = PART / (F * 2)

    adj_pairs = adj_t.rearrange("(i k p) m -> i p k m", p=P, k=2)
    x_pairs = x.rearrange("(i k) p n -> i p k n", k=2)

    with ExitStack() as ctx:
        def sb(name, shape, dt=F32):
            return ctx.enter_context(nc.sbuf_tensor(name, shape, dt))

        def sem(name):
            return ctx.enter_context(nc.semaphore(name))

        G = sb("G", [P, 3, 2 * M, HC])
        work = sb("work", [P, 4 * N])
        stage = [work[:, h * 2 * N:(h + 1) * 2 * N].rearrange("p (k m) -> p k m", k=2) for h in range(2)]
        Zt = sb("Zt", [P, 2, 2, M, HC], F16)
        Z2 = work[:, :].bitcast(F16).rearrange("p (e m n) -> p e m n", e=2, m=M)
        Zh = [Zt[:, 0, 0], Zt[:, 1, 0], Z2[:, 0]]
        Zl = [Zt[:, 0, 1], Zt[:, 1, 1], Z2[:, 1]]
        ATh_all = sb("ATh", [P, M * DIAG], F16)
        ATl_all = sb("ATl", [P, M * DIAG], F16)
        ATh, ATl = (t[:, 0:M * N].rearrange("p (k m) -> p k m", k=M) for t in (ATh_all, ATl_all))
        ATh_diag, ATl_diag = (t[:, :].rearrange("p (k m) -> p k m", m=DIAG)[:, :, 0:P]
                              for t in (ATh_all, ATl_all))
        ADh = sb("ADh", [P, M, P], F16)
        ADl = sb("ADl", [P, M, P], F16)
        xn = [sb(f"xn{u}", [P, HC]) for u in range(2)]
        hTh = [sb(f"hTh{u}", [P, HC], F16) for u in range(2)]
        hTl = [sb(f"hTl{u}", [P, HC], F16) for u in range(2)]
        w0_in = sb("w0_in", [P, 3, F])
        w1_in = sb("w1_in", [P, 7, F])
        wcat = [w0_in, w1_in]
        Wh = [sb(f"Wh{i}", [P, NB[i] * F], F16) for i in range(2)]
        Wl = [sb(f"Wl{i}", [P, NB[i] * F], F16) for i in range(2)]
        ident = sb("ident", [P, P])
        offdiag = sb("offdiag", [P, P], F16)
        bias_b = sb("bias_b", [P, F])
        junk = [Zh[1][:, 2 * v:2 * v + N // HC, :].rearrange("p m n -> p (m n)") for v in range(2)]

        bn6 = sb("bn6", [P, 2, HB, 6])
        moments = sb("moments", [P, 2, HB, 2])
        var, sd, r0, nt, nt2, rstd, shift = (sb(n, [P, 2, HB]) for n in "var sd r0 nt nt2 rstd shift".split())
        wmax = sb("wmax", [P, 2])
        wgmax = sb("wgmax", [P, 2])
        wscale = sb("wscale", [P, 2])
        wback = sb("wback", [P, 2])
        asum = [sb(f"asum{h}", [P, 2]) for h in range(2)]
        ascale = [sb(f"ascale{h}", [P, 2]) for h in range(2)]
        aback = sb("aback", [P, M])
        abackb = sb("abackb", [P, M], BF16)
        avec = sb("avec", [P, 2, M])
        dinv = sb("dinv", [P, M])
        first_root = sb("first_root", [P, 1])
        frow = sb("frow", [P, 2, M])
        fmax = sb("fmax", [P, 2])
        fgmax = sb("fgmax", [P, 2])
        zw = sb("zw", [P, 2, M])
        zscale0 = sb("zscale0", [P, M])
        alpha0 = sb("alpha0", [P, 2, M])
        fb = sb("fb", [P, 4])
        positive, deg, root_in, root, d0, d1, d2, dp, pback = (
            sb(n, [P, M]) for n in "positive deg root_in root d0 d1 d2 dp pback".split())
        tmax = sb("tmax", [P, 2, M])
        dmax = sb("dmax", [P, 2, M])
        hmax = sb("hmax", [P, 2])
        hgmax = sb("hgmax", [P, 2])
        zscale = sb("zscale", [P, 2, M])
        zback = sb("zback", [P, 2])
        alpha = sb("alpha", [P, 2, M])
        pw = sb("pw", [P, 16, 6])

        psA = ctx.enter_context(nc.psum_tensor("psA", [P, 2, 512], F32))
        psT = ctx.enter_context(nc.psum_tensor("psT", [P, 2, 512], F32))
        psW = ctx.enter_context(nc.psum_tensor("psW", [P, HB, 512], F32))
        deg_ps = psA[:, 0, 0:M]

        adj_in = [sem(f"adj_in{u}") for u in range(2)]
        adj_first = sem("adj_first")
        x_in = [sem(f"x_in{u}") for u in range(2)]
        names = """w_in0 w_in1 bias_in out_done consts w_combined w_max w_gmax w_scale w_hi w_lo pow2_step
            a_sum a_scale at_hi at_lo ad_copied at_masked degrees deg_read frow_ready dinv_step f_step f_max f_gmax
            f_scaled ln_stats ln_moments ln_var ln_sd ln_r0 ln_n1 ln_n2 ln_rstd ln_shift xn_done xT_done
            hT_hi hT_lo hw_done cols_done psW_free bias_added row_max mm_done bank_free
            hm_step half_max half_gmax scale_ready z_hi z_lo zc_lo diag_hi diag_lo""".split()
        S = {n: sem(n) for n in names}
        (w_in0, w_in1, bias_in, out_done, consts, w_combined, w_max, w_gmax, w_scale, w_hi, w_lo, pow2_step,
         a_sum, a_scale, at_hi, at_lo, ad_copied, at_masked, degrees, deg_read, frow_ready, dinv_step, f_step, f_max,
         f_gmax, f_scaled, ln_stats, ln_moments, ln_var, ln_sd, ln_r0, ln_n1, ln_n2, ln_rstd, ln_shift,
         xn_done, xT_done, hT_hi, hT_lo, hw_done, cols_done, psW_free, bias_added, row_max, mm_done,
         bank_free, hm_step, half_max, half_gmax, scale_ready, z_hi, z_lo, zc_lo, diag_hi,
         diag_lo) = (S[n] for n in names)

        def tile(j, t):
            return G[:, j, t, :]

        def by_batch(ap):
            return ap.rearrange("p (b f) -> p b f", f=F)

        def two_batches(ap, e):
            return by_batch(ap)[:, 2 * e:2 * e + 2, :]

        TARGET = [1, 0, 2, 1, 0]
        SOURCE = {0: 2, 2: 1, 3: 1, 6: 2, 7: 2, 8: 1, 9: 1}
        SPLIT_NO = {0: 0, 2: 1, 3: 2, 6: 3, 7: 4, 8: 5, 9: 6}

        def tiles_split(q):
            return 0 if q == 0 else EARLY + M * (SPLIT_NO[q] - 1)

        def parts_from_psum(tiles):
            return 2 * (tiles - EARLY)

        block = ctx.enter_context(nc.Block())

        @block.sync
        def _(sp):
            def load_x(i):
                if i >= 2:
                    sp.wait_ge(x_in[i % 2], 16 * (i // 2))
                sp.dma_start(G[:, 0, 2 * i:2 * i + 2, :], x_pairs[i]).then_inc(x_in[i % 2], 16)

            def load_adj(i):
                if i >= 2:
                    sp.wait_ge(at_lo, 2 * (i - 1))
                if i == 0:
                    for k, tile_in in ((0, adj_first), (1, adj_in[0])):
                        sp.dma_start(stage[0][:, k, :], adj_pairs[0][:, k, :]).then_inc(tile_in, 16)
                else:
                    sp.dma_start(stage[i % 2], adj_pairs[i]).then_inc(adj_in[i % 2], 16)

            load_adj(0)
            load_adj(1)
            sp.dma_start(w0_in[:, :, :], w0.rearrange("k i o -> i k o")).then_inc(w_in0, 16)
            load_x(0)
            load_x(1)
            sp.dma_start(bias_b[:, :], bias.partition_broadcast(P)).then_inc(bias_in, 16)
            load_x(2)
            for i in range(2, LOADS):
                load_adj(i)
            for i in range(3, 2 * LOADS):
                load_x(i)
            sp.dma_start(w1_in[:, :, :], w1.rearrange("k i o -> i k o")).then_inc(w_in1, 16)
            with sp.Fori(0, 2 * M) as t:
                sp.wait_ge(bank_free, t + 8 * M + 3)
                sp.dma_start(out[t], tile(0, t)).then_inc(out_done, 16)
            sp.wait_ge(out_done, 16 * 2 * M)

        @block.gpsimd
        def _(pool):
            nc.gpsimd.memset(ident[:, :], 0.0).then_inc(consts, 1)
            nc.gpsimd.memset(offdiag[:, :], 1.0).then_inc(consts, 1)
            pool.wait_ge(consts, 2)
            for t, v in ((ident, 1.0), (offdiag, 0.0)):
                nc.gpsimd.affine_select(out=t[:, :], in_=t[:, :], compare_op=ALU.not_equal, fill=v, base=0,
                                        pattern=[[-1, P]], channel_multiplier=1).then_inc(consts, 1)
            pool.wait_ge(w_max, 1)
            nc.gpsimd.partition_all_reduce(wgmax[:, 0:1], wmax[:, 0:1], P, ABSMAX).then_inc(w_gmax, 1)
            pool.wait_ge(consts, 4)
            pool.wait_ge(bias_in, 16)

            def add_bias(t):
                pool.wait_ge(xn_done, t + 1)
                pool.nop(nofuse=True)
                nc.gpsimd.tensor_tensor(by_batch(tile(0, t)), by_batch(tile(0, t)),
                                        bias_b[:, :].unsqueeze(1).broadcast_to([P, HB, F]), ALU.add).then_inc(bias_added, 1)

            def keep(k, at, ad, ready):
                pool.wait_ge(ready, k + 1)
                nc.gpsimd.tensor_copy(ad[:, k, :], at[:, k, :]).then_inc(ad_copied, 1)

            def mask(k, copies):
                pool.wait_ge(ad_copied, copies)
                pool.nop(nofuse=True)
                for at in (ATh_diag, ATl_diag):
                    last = nc.gpsimd.tensor_tensor(at[:, k, :], at[:, k, :], offdiag[:, :], ALU.mult)
                last.then_inc(at_masked, 1)

            high, low = (ATh_diag, ADh, at_hi), (ATl_diag, ADl, at_lo)
            with pool.Fori(0, M - 2) as k:
                keep(k, *high)
                keep(k, *low)
                mask(k, 2 * k + 2)
            for k in (M - 2, M - 1):
                keep(k, *high)
            for k in (M - 2, M - 1):
                keep(k, *low)
                mask(k, M + k + 1)
            for t in range(4):
                add_bias(t)
            pool.wait_ge(f_max, 1)
            for i in range(2):
                nc.gpsimd.partition_all_reduce(fgmax[:, i:i + 1], fmax[:, i:i + 1], P, ABSMAX).then_inc(f_gmax, 1)
            with pool.Fori(4, 2 * M) as t:
                add_bias(t)
            pool.wait_ge(w_max, 2)
            nc.gpsimd.partition_all_reduce(wgmax[:, 1:2], wmax[:, 1:2], P, ABSMAX).then_inc(w_gmax, 1)
            for n, q in enumerate(q for q in SPLIT_NO if q):
                pool.wait_ge(half_max, n + 1)
                c = q % 2
                nc.gpsimd.partition_all_reduce(hgmax[:, c:c + 1], hmax[:, c:c + 1], P, ABSMAX).then_inc(half_gmax, 1)

        @block.scalar
        def _(act):
            def deviation(call, v):
                act.wait_ge(ln_var, call + 1)
                nc.scalar.activation(sd[:, v, :], var[:, v, :], ACT.Sqrt).then_inc(ln_sd, 1)

            def normalise(tiles):
                for t, u in tiles:
                    for b in range(HB):
                        last = nc.scalar.activation(xn[u][:, b * F:(b + 1) * F], tile(0, t)[:, b * F:(b + 1) * F],
                                                    ACT.Identity, scale=rstd[:, u, b:b + 1], bias=shift[:, u, b:b + 1])
                    last.then_inc(xn_done, 1)

            def transposed_hi(j, u):
                act.wait_ge(xT_done, j + 1)
                nc.scalar.activation(hTh[u][:, :], psT[:, u, :], ACT.Relu).then_inc(hT_hi, 1)

            def columns(j, t, layer, z=None, m=None, halves=(0, 1)):
                k = NB[layer] - 1
                addends = slice(F, (k if z is not None else k + 1) * F)
                for e in halves:
                    act.wait_ge(hw_done, 2 * j + e + 1)
                    if z is not None:
                        nc.scalar.activation(two_batches(Zh[z][:, m, :], e), psW[:, 2 * e:2 * e + 2, k * F:(k + 1) * F],
                                             ACT.Copy, scale=zw[:, layer, bass.ds(m, 1)])
                    ps = psW[:, 2 * e:2 * e + 2, addends].rearrange("p b (k f) -> p k b f", f=F)
                    to = G[:, 1:1 + ps.shape[1], t, 2 * e * F:2 * (e + 1) * F].rearrange("p k (b f) -> p k b f", f=F)
                    nc.scalar.activation(to, ps, ACT.Copy, scale=wback[:, layer:layer + 1]).then_inc(cols_done, 1)

            def weights_hi(layer):
                act.wait_ge(w_scale, layer + 1)
                nc.scalar.activation(Wh[layer][:, :], wcat[layer][:, 0:NB[layer], :].rearrange("p k o -> p (k o)"),
                                     ACT.Copy, scale=wscale[:, layer:layer + 1]).then_inc(w_hi, 1)

            def split_hi_tile(q, m):
                c = q % 2
                scale = zscale0[:, :] if q == 0 else zscale[:, c, :]
                nc.scalar.activation(Zh[q % 3][:, m, :], tile(SOURCE[q], m + c * M), ACT.Copy,
                                     scale=scale[:, bass.ds(m, 1)]).then_inc(z_hi, 1)

            def split_hi(q):
                act.wait_ge(scale_ready, SPLIT_NO[q] + 1)
                with act.Fori(0, M) as m:
                    split_hi_tile(q, m)

            def column_sums(r):
                if r:
                    act.wait_ge(adj_in[r % 2], 16 * (r // 2 + 1))
                for v in range(2):
                    if r == 0:
                        act.wait_ge((adj_first, adj_in[0])[v], 16)
                    last = nc.scalar.activation(junk[v], stage[r % 2][:, v, :], ACT.Abs, accum_out=asum[r % 2][:, v:v + 1])
                last.then_inc(a_sum, 1)

            def adjacency_hi(r):
                act.wait_ge(a_scale, r + 1)
                for v in range(2):
                    nc.scalar.activation(ATh[:, 2 * r + v, :], stage[r % 2][:, v, :], ACT.Copy,
                                         scale=ascale[r % 2][:, v:v + 1]).then_inc(at_hi, 1)

            act.wait_ge(bank_free, 2)
            nc.scalar.activation(first_root[:, :], avec[:, 1, 0:1], ACT.Sqrt)
            column_sums(0)
            adjacency_hi(0)
            column_sums(1)
            adjacency_hi(1)
            deviation(0, slice(0, 2))
            column_sums(2)
            act.wait_ge(ln_shift, 1)
            normalise([(0, 0), (1, 1)])
            adjacency_hi(2)
            weights_hi(0)
            transposed_hi(0, 0)
            column_sums(3)
            transposed_hi(1, 1)
            deviation(1, slice(0, 2))
            adjacency_hi(3)
            act.wait_ge(ln_shift, 2)
            normalise([(2, 0), (3, 1)])
            deviation(2, slice(0, 2))
            for r in range(1, 2 * LOADS + 1):
                def finish(v):
                    t = 2 * (r - 1) + v
                    z, m = (t // M, t % M) if t >= EARLY else (None, None)
                    columns(t, t, 0, z, m)

                def transposed(v):
                    if r < 2 * LOADS:
                        transposed_hi(2 * r + v, v)

                def normalise_next(v):
                    if r < 2 * LOADS - 1:
                        if v == 0:
                            act.wait_ge(ln_shift, r + 2)
                        normalise([(2 * (r + 1) + v, v)])

                if r == 2:
                    act.wait_ge(f_scaled, 1)
                finish(0)
                transposed(0)
                if r == 2:
                    deviation(3, slice(0, 2))
                if r == 1:
                    act.wait_ge(dinv_step, 1)
                    nc.scalar.activation(root[:, :], root_in[:, :], ACT.Sqrt).then_inc(dinv_step, 1)
                normalise_next(0)
                finish(1)
                transposed(1)
                if r == 1:
                    act.wait_ge(scale_ready, 1)
                    act.wait_ge(cols_done, 2 * EARLY)
                    for m in range(EARLY):
                        split_hi_tile(0, m)
                normalise_next(1)
                if 1 < r < 2 * LOADS - 2:
                    deviation(r + 2, slice(0, 2))
            weights_hi(1)
            split_hi(2)

            def follow(c, m, u, last=False):
                j = m - 1 + J1 + c * M
                finished = (j, m - 1 + c * M, 1, (4 + c) % 3, m - 1)
                transposed_hi(j, 1 - u)
                deviation(j + 1 - J1 + 2 * LOADS, u)
                columns(*finished, halves=(0,))
                act.wait_ge(ln_shift, j + 1 - J1 + 2 * LOADS + 1)
                normalise([(m + c * M, u)])
                if c == 1 and last:
                    act.wait_ge(mm_done, 4 * M)
                    nc.scalar.copy(ATh_diag, ADh[:, :, :]).then_inc(diag_hi, 1)
                columns(*finished, halves=(1,))
                if c == 0 and not last:
                    split_hi_tile(3, m + 1)

            for c in range(2):
                if c == 0:
                    deviation(2 * LOADS, 0)
                    act.wait_ge(ln_shift, 2 * LOADS + 1)
                    normalise([(0, 0)])
                    act.wait_ge(f_scaled, 3)
                    act.wait_ge(scale_ready, SPLIT_NO[3] + 1)
                    for m in range(2):
                        split_hi_tile(3, m)
                else:
                    transposed_hi(J1 + M - 1, 1)
                    deviation(2 * LOADS + M, 0)
                    columns(J1 + M - 1, M - 1, 1, 1, M - 1)
                    act.wait_ge(ln_shift, 2 * LOADS + M + 1)
                    normalise([(M, 0)])
                with act.Fori(0, LOADS - 1) as i:
                    follow(c, 2 * i + 1, 1)
                    follow(c, 2 * i + 2, 0)
                follow(c, M - 1, 1, last=True)
            transposed_hi(J1 + 2 * M - 1, 1)
            columns(J1 + 2 * M - 1, 2 * M - 1, 1, 2, M - 1)
            for q in (6, 7, 8, 9):
                split_hi(q)

        @block.tensor
        def _(pe):
            def products(q, m, bank, ks, first=0, final=M - 1):
                zh, zl = Zh[q % 3], Zl[q % 3]
                for k in ks:
                    for a, z in ((ATh, zh), (ATh, zl), (ATl, zh)):
                        last = nc.tensor.matmul(psA[:, bank, :], a[:, k, bass.ts(m, P)], z[:, k, :],
                                                start=(k == first and z is zh and a is ATh),
                                                stop=(k == final and a is ATl))
                if ks[-1] == final:
                    last.then_inc(mm_done, 1)

            def chain_transpose(j, u):
                pe.wait_ge(xn_done, j + 1)
                pe.wait_ge(hT_lo, j + 1)
                for b in range(HB):
                    last = nc.tensor.transpose(psT[:, u, b * F:(b + 1) * F], xn[u][:, b * F:(b + 1) * F], ident[:, :])
                last.then_inc(xT_done, 1)

            def chain_weights(j, u, layer):
                pe.wait_ge(hT_hi, j + 1)
                n = NB[layer] * F
                for e in range(2):
                    pe.wait_ge(psW_free, 2 * j + e + 1)
                    for b in (2 * e, 2 * e + 1):
                        for w in (Wh, Wl):
                            nc.tensor.matmul(psW[:, b, 0:n], hTh[u][:, b * F:(b + 1) * F], w[layer][:, :],
                                             start=(w is Wh), stop=False)
                    pe.wait_ge(hT_lo, j + 3)
                    for b in (2 * e, 2 * e + 1):
                        last = nc.tensor.matmul(psW[:, b, 0:n], hTl[u][:, b * F:(b + 1) * F], Wh[layer][:, :],
                                                start=False, stop=True)
                    last.then_inc(hw_done, 1)

            def slot(q, m, bank):
                pe.wait_ge(bank_free, m + q * M + 1)
                products(q, m, bank, range(M))

            def slot_with_chain(q, m, bank, j, u, last_tile=None):
                pe.wait_ge(bank_free, m + q * M + 1)
                products(q, m, bank, range(M - 2))
                chain_transpose(j, u)
                products(q, m, bank, range(M - 2, M - 1))
                if last_tile is not None:
                    pe.wait_ge(z_lo, last_tile)
                products(q, m, bank, range(M - 1, M))
                chain_weights(j, u, 1)

            pe.wait_ge(consts, 4)

            def pair_transpose(r):
                for v in range(2):
                    chain_transpose(2 * r + v, v)

            def tile_degrees(k):
                pe.wait_ge(at_masked, k + 1)
                for a in (ATh, ATl):
                    for m in range(M):
                        last = nc.tensor.matmul(deg_ps[:, m:m + 1], a[:, k, m * P:(m + 1) * P], abackb[:, k:k + 1],
                                                start=(k == 0 and m == 0 and a is ATh),
                                                stop=(k == M - 1 and m == M - 1 and a is ATl))
                last.then_inc(degrees, 1)

            def first_slots(k):
                if k < EARLY:
                    pe.wait_ge(z_lo, k + 1)
                else:
                    pe.wait_ge(zc_lo, parts_from_psum(k + 1))
                for m in range(2):
                    products(0, m, m, range(k, k + 1))

            for k in range(3):
                tile_degrees(k)
            pair_transpose(0)
            for k in range(3, M - 3):
                tile_degrees(k)
            pe.wait_ge(w_lo, 1)
            chain_weights(0, 0, 0)
            tile_degrees(M - 3)
            chain_transpose(2, 0)
            tile_degrees(M - 2)
            chain_transpose(3, 1)
            tile_degrees(M - 1)
            chain_weights(1, 1, 0)
            chain_weights(2, 0, 0)
            pe.wait_ge(deg_read, 3)
            pe.wait_ge(bank_free, 2)
            for r in range(2, LOADS + 1):
                for v in range(2):
                    chain_transpose(2 * r + v, v)
                    if r == 2:
                        first_slots(v)
                chain_weights(2 * r - 1, 1, 0)
                first_slots(2 * r - 2)
                chain_weights(2 * r, 0, 0)
                if r < LOADS:
                    first_slots(2 * r - 1)
            for m in range(2, LOADS + 2):
                r = LOADS - 1 + m
                if r < 2 * LOADS:
                    pair_transpose(r)
                before = M // 2
                if m == 2:
                    first_slots(M - 1)
                    before = 0
                else:
                    pe.wait_ge(bank_free, m + 1)
                    products(0, m, m % 2, range(before))
                chain_weights(2 * r - 1, 1, 0)
                if m == 2:
                    pe.wait_ge(bank_free, m + 1)
                products(0, m, m % 2, range(before, M))
                if r < 2 * LOADS:
                    chain_weights(2 * r, 0, 0)
            for m in range(LOADS + 2, M):
                slot(0, m, m % 2)
            pe.wait_ge(zc_lo, parts_from_psum(2 * M))
            with pe.Fori(0, LOADS) as i:
                for u in range(2):
                    slot(1, 2 * i + u, u)
            pe.wait_ge(w_lo, 2)
            for c in range(2):
                q = 2 + c
                z_all = tiles_split(q) + M
                if c == 0:
                    pe.wait_ge(z_lo, z_all)
                    slot(q, 0, 0)
                    slot(q, 1, 1)
                    chain_transpose(J1, 0)
                    pe.wait_ge(bank_free, 2 + q * M + 1)
                    products(q, 2, 0, range(2))
                    chain_weights(J1, 0, 1)
                    products(q, 2, 0, range(2, M - 2))
                    chain_transpose(J1 + 1, 1)
                    products(q, 2, 0, range(M - 2, M))
                    chain_weights(J1 + 1, 1, 1)
                else:
                    pe.wait_ge(z_lo, z_all - 1)
                    slot_with_chain(q, 0, 0, J1 + M - 1, 1, last_tile=z_all)
                    slot_with_chain(q, 1, 1, J1 + M, 0)
                    slot_with_chain(q, 2, 0, J1 + M + 1, 1)
                with pe.Fori(1, LOADS - 1) as i:
                    for u in (1, 0):
                        m = 2 * i + (1 if u else 2)
                        slot_with_chain(q, m, u, m - 1 + J1 + c * M, 1 - u)
                slot_with_chain(q, M - 1, 1, M - 2 + J1 + c * M, 0)
            pe.wait_ge(zc_lo, parts_from_psum(3 * M))
            pe.wait_ge(bank_free, 4 * M + 1)
            products(4, 0, 0, range(1, M - 1), first=1, final=0)
            chain_transpose(J1 + 2 * M - 1, 1)
            products(4, 0, 0, range(M - 1, M), first=1, final=0)
            pe.wait_ge(diag_hi, 1)
            pe.wait_ge(diag_lo, 1)
            products(4, 0, 0, range(1), first=1, final=0)
            chain_weights(J1 + 2 * M - 1, 1, 1)
            with pe.Fori(0, LOADS - 1) as i:
                for u in (1, 0):
                    slot(4, 2 * i + (1 if u else 2), u)
            slot(4, M - 1, 1)
            for q in range(5, 10):
                if q == 5:
                    pe.wait_ge(zc_lo, parts_from_psum(4 * M))
                else:
                    pe.wait_ge(z_lo, tiles_split(q) + M)
                with pe.Fori(0, LOADS) as i:
                    for u in range(2):
                        slot(q, 2 * i + u, u)

        @block.vector
        def _(dve):
            def powers(src, n, w, call):
                t = pw[:, n, :]
                nc.vector.tensor_scalar(t[:, 0:w], src, TINY, None, ALU.max).then_inc(pow2_step, 1)
                dve.wait_ge(pow2_step, 3 * call + 1)
                nc.vector.tensor_scalar(t[:, 2:2 + w].bitcast(I32), t[:, 0:w].bitcast(I32), EXPONENT, None,
                                        ALU.bitwise_and).then_inc(pow2_step, 1)
                dve.wait_ge(pow2_step, 3 * call + 2)
                nc.vector.reciprocal(t[:, 4:4 + w], t[:, 2:2 + w]).then_inc(pow2_step, 1)
                dve.wait_ge(pow2_step, 3 * call + 3)
                return t[:, 2:2 + w], t[:, 4:4 + w]

            CALL = {"w0": 3, "f0": 1 + LOADS, "w1": 2 + LOADS, 2: 3 + LOADS, "f1": 4 + LOADS,
                    3: 5 + LOADS, 6: 6 + LOADS, 7: 7 + LOADS, 8: 8 + LOADS, 9: 9 + LOADS}
            SLOT_OF_PW = {k: n for n, k in enumerate(["a0", "a1", *CALL])}

            def weights_cat(layer):
                return wcat[layer][:, 0:NB[layer], :].rearrange("p k o -> p (k o)")

            def weights_maximum(layer):
                dve.wait_ge(w_combined, 2 * layer + 1)
                if layer == 0:
                    dve.wait_ge(w_combined, 2)
                nc.vector.tensor_reduce(wmax[:, layer:layer + 1], weights_cat(layer), AX.X, ALU.max,
                                        apply_absolute_value=True).then_inc(w_max, 1)

            def weights_scale(layer):
                dve.wait_ge(w_gmax, layer + 1)
                p, rp = powers(wgmax[:, layer:layer + 1], SLOT_OF_PW[f"w{layer}"], 1, CALL[f"w{layer}"])
                nc.vector.tensor_scalar(wback[:, layer:layer + 1], p, 1.0 / (PART * H_SCALE), None, ALU.mult)
                nc.vector.tensor_scalar(wscale[:, layer:layer + 1], rp, PART, None, ALU.mult).then_inc(w_scale, 1)

            def weights_lo(layer):
                dve.wait_ge(w_scale, layer + 1)
                dve.wait_ge(w_hi, layer + 1)
                nc.vector.scalar_tensor_tensor(Wl[layer][:, :], weights_cat(layer), wscale[:, layer:layer + 1],
                                               Wh[layer][:, :], ALU.mult, ALU.subtract).then_inc(w_lo, 1)

            def row_statistics(call, tiles):
                dve.nop(nofuse=True)
                for t, u in tiles:
                    for b in range(HB):
                        last = nc.vector.bn_stats(bn6[:, u, b, :], tile(0, t)[:, b * F:(b + 1) * F])
                last.then_inc(ln_stats, 1)

            def mean_and_variance(call, tiles, v):
                dve.wait_ge(ln_stats, call + 1)
                dve.nop(nofuse=True)
                for t, u in tiles:
                    for b in range(HB):
                        last = nc.vector.bn_aggr(moments[:, u, b, :], bn6[:, u, b, :])
                last.then_inc(ln_moments, 1)
                dve.wait_ge(ln_moments, call + 1)
                nc.vector.tensor_scalar(var[:, v, :], moments[:, v, :, 1], EPS, None, ALU.add).then_inc(ln_var, 1)

            def statistics(call, tiles, v):
                row_statistics(call, tiles)
                mean_and_variance(call, tiles, v)

            def factors(call, v):
                dve.wait_ge(ln_sd, call + 1)
                nc.vector.reciprocal(r0[:, v, :], sd[:, v, :]).then_inc(ln_r0, 1)
                dve.wait_ge(ln_r0, call + 1)
                nc.vector.tensor_tensor(nt[:, v, :], r0[:, v, :], var[:, v, :], ALU.mult).then_inc(ln_n1, 1)
                dve.wait_ge(ln_n1, call + 1)
                nc.vector.scalar_tensor_tensor(nt2[:, v, :], nt[:, v, :], -0.5 * H_SCALE, r0[:, v, :],
                                               ALU.mult, ALU.mult).then_inc(ln_n2, 1)
                dve.wait_ge(ln_n2, call + 1)
                nc.vector.scalar_tensor_tensor(rstd[:, v, :], nt2[:, v, :], 1.5 * H_SCALE, r0[:, v, :],
                                               ALU.add, ALU.mult).then_inc(ln_rstd, 1)
                dve.wait_ge(ln_rstd, call + 1)
                nc.vector.scalar_tensor_tensor(shift[:, v, :], moments[:, v, :, 0], -1.0, rstd[:, v, :],
                                               ALU.mult, ALU.mult).then_inc(ln_shift, 1)

            def transposed_lo(j, u):
                dve.wait_ge(hT_hi, j + 1)
                nc.vector.scalar_tensor_tensor(hTl[u][:, :], psT[:, u, :], 0.0, hTh[u][:, :],
                                               ALU.max, ALU.subtract).then_inc(hT_lo, 1)

            def first_columns(j, t, layer, z=None, m=None, halves=(0, 1)):
                for e in halves:
                    dve.wait_ge(cols_done, 2 * j + e + 1)
                    if z is not None:
                        k = NB[layer] - 1
                        nc.vector.scalar_tensor_tensor(two_batches(Zl[z][:, m, :], e),
                                                       psW[:, 2 * e:2 * e + 2, k * F:(k + 1) * F],
                                                       zw[:, layer, bass.ds(m, 1)], two_batches(Zh[z][:, m, :], e),
                                                       ALU.mult, ALU.subtract).then_inc(zc_lo, 1)
                    if layer == 0:
                        dve.wait_ge(bias_added, j + 1)
                    nc.vector.scalar_tensor_tensor(two_batches(tile(0, t), e), psW[:, 2 * e:2 * e + 2, 0:F],
                                                   wback[:, layer:layer + 1], two_batches(tile(0, t), e),
                                                   ALU.mult, ALU.add).then_inc(psW_free, 1)

            def evacuate(q, m, bank):
                p, c = q // 2, q % 2
                g = m + q * M
                t = tile(TARGET[p], m + c * M)
                back = alpha0[:, p // 2, :] if p in (0, 2) else alpha[:, c, :]
                dve.wait_ge(mm_done, g + 1)
                nc.vector.scalar_tensor_tensor(t, psA[:, bank, :], back[:, bass.ds(m, 1)], t,
                                               ALU.mult, ALU.add).then_inc(bank_free, 1)
                if p in (0, 2, 3):
                    dve.wait_ge(bank_free, g + 3)
                    nc.vector.tensor_reduce(tmax[:, c, bass.ds(m, 1)], t, AX.X, ALU.max,
                                            apply_absolute_value=True).then_inc(row_max, 1)

            def half_maximum(q):
                c, layer, n = q % 2, int(q >= 4), SPLIT_NO[q]
                dve.wait_ge(row_max, M * n)
                nc.vector.tensor_tensor(dmax[:, c, :], tmax[:, c, :], frow[:, layer, :], ALU.mult).then_inc(hm_step, 1)
                dve.wait_ge(hm_step, 2 * n - 1)
                nc.vector.tensor_reduce(hmax[:, c:c + 1], dmax[:, c, :], AX.X, ALU.max,
                                        apply_absolute_value=True).then_inc(half_max, 1)

            def half_scale(q):
                c, layer, n = q % 2, int(q >= 4), SPLIT_NO[q]
                dve.wait_ge(half_gmax, n)
                pq, rp = powers(hgmax[:, c:c + 1], SLOT_OF_PW[q], 1, CALL[q])
                nc.vector.tensor_scalar(zscale[:, c, :], frow[:, layer, :], rp, PART, ALU.mult,
                                        ALU.mult).then_inc(scale_ready, 1)
                nc.vector.tensor_scalar(zback[:, c:c + 1], pq, 1.0 / PART, None, ALU.mult).then_inc(hm_step, 1)
                dve.wait_ge(hm_step, 2 * n)
                nc.vector.tensor_scalar(alpha[:, c, :], avec[:, layer, :], zback[:, c:c + 1], None, ALU.mult)
                dve.wait_ge(scale_ready, n + 1)

            def split_lo_tile(q, m):
                c = q % 2
                scale = zscale0[:, :] if q == 0 else zscale[:, c, :]
                dve.wait_ge(z_hi, m + tiles_split(q) + 1)
                nc.vector.scalar_tensor_tensor(Zl[q % 3][:, m, :], tile(SOURCE[q], m + c * M),
                                               scale[:, bass.ds(m, 1)], Zh[q % 3][:, m, :],
                                               ALU.mult, ALU.subtract).then_inc(z_lo, 1)

            def split_lo(q, first, n):
                with dve.Fori(first, first + n) as m:
                    split_lo_tile(q, m)

            def layer_scale(layer):
                dve.wait_ge(f_gmax, layer + 1)
                wp = pw[:, SLOT_OF_PW[f"w{layer}"], :]
                pf, rpf = powers(fgmax[:, layer:layer + 1], SLOT_OF_PW[f"f{layer}"], 1, CALL[f"f{layer}"])
                f = fb[:, 2 * layer:2 * layer + 1]
                b = fb[:, 2 * layer + 1:2 * layer + 2]
                nc.vector.tensor_scalar(f, rpf, wp[:, 4:5], BOUND, ALU.mult, ALU.mult).then_inc(f_step, 1)
                nc.vector.tensor_scalar(b, pf, wp[:, 2:3], 1.0 / BOUND, ALU.mult, ALU.mult).then_inc(f_step, 1)
                dve.wait_ge(f_step, 2 * layer + 2)
                if layer == 0:
                    nc.vector.tensor_scalar(zscale0[:, :], frow[:, 0, :], f, None, ALU.mult).then_inc(scale_ready, 1)
                nc.vector.tensor_scalar(zw[:, layer, :], frow[:, layer, :], f, wback[:, layer:layer + 1],
                                        ALU.mult, ALU.mult).then_inc(f_scaled, 1)
                nc.vector.tensor_scalar(alpha0[:, layer, :], avec[:, layer, :], b, None, ALU.mult).then_inc(f_scaled, 1)
                dve.wait_ge(f_scaled, 2 * layer + 2)

            nc.vector.memset(avec[:, 1, :], 1.0).then_inc(bank_free, 2)
            nc.vector.memset(tmax[:, :, :], 0.0).then_inc(hT_lo, 2)
            nc.vector.memset(pw[:, 15, :], 0.0).then_inc(psW_free, 2)

            def degree_factors():
                dve.wait_ge(degrees, M)
                nc.vector.tensor_scalar(positive[:, :], deg_ps, 0.0, None, ALU.is_gt).then_inc(deg_read, 1)
                nc.vector.tensor_scalar(root_in[:, :], deg_ps, 0.0, None, ALU.is_le).then_inc(deg_read, 1)
                dve.wait_ge(deg_read, 2)
                nc.vector.tensor_tensor(deg[:, :], positive[:, :], deg_ps, ALU.mult).then_inc(deg_read, 1)
                dve.wait_ge(deg_read, 3)
                nc.vector.tensor_tensor(root_in[:, :], root_in[:, :], deg[:, :], ALU.add).then_inc(dinv_step, 1)
                nc.vector.tensor_tensor(pback[:, :], positive[:, :], aback[:, :], ALU.mult)
                nc.vector.tensor_copy(frow[:, 1, :], aback[:, :]).then_inc(frow_ready, 1)
                dve.wait_ge(frow_ready, 1)
                nc.vector.tensor_reduce(fmax[:, 1:2], frow[:, 1, :], AX.X, ALU.max)
                dve.wait_ge(dinv_step, 2)
                nc.vector.reciprocal(d0[:, :], root[:, :]).then_inc(dinv_step, 1)
                dve.wait_ge(dinv_step, 3)
                nc.vector.tensor_tensor(d1[:, :], d0[:, :], root_in[:, :], ALU.mult).then_inc(dinv_step, 1)
                nc.vector.tensor_tensor(dp[:, :], d0[:, :], pback[:, :], ALU.mult)
                nc.vector.tensor_tensor(positive[:, :], d0[:, :], positive[:, :], ALU.mult)
                dve.wait_ge(dinv_step, 4)
                nc.vector.scalar_tensor_tensor(d2[:, :], d1[:, :], -0.5, d0[:, :], ALU.mult, ALU.mult).then_inc(dinv_step, 1)
                dve.wait_ge(dinv_step, 5)
                nc.vector.scalar_tensor_tensor(frow[:, 0, :], d2[:, :], 1.5, dp[:, :], ALU.add,
                                               ALU.mult).then_inc(frow_ready, 1)
                nc.vector.scalar_tensor_tensor(dinv[:, :], d2[:, :], 1.5, positive[:, :], ALU.add,
                                               ALU.mult).then_inc(dinv_step, 1)
                dve.wait_ge(frow_ready, 2)
                nc.vector.tensor_reduce(fmax[:, 0:1], frow[:, 0, :], AX.X, ALU.max).then_inc(f_max, 1)
                dve.wait_ge(dinv_step, 6)
                nc.vector.tensor_scalar(avec[:, 0, :], dinv[:, :], -1.0, None, ALU.mult)

            def pair_rows(r):
                dve.wait_ge(x_in[r % 2], 16 * (r // 2 + 1))
                row_statistics(r, [(2 * r, 0), (2 * r + 1, 1)])

            def pair_moments(r):
                mean_and_variance(r, [(2 * r, 0), (2 * r + 1, 1)], slice(0, 2))

            def pair_statistics(r):
                pair_rows(r)
                pair_moments(r)

            def column_scales(r):
                h = r % 2
                dve.wait_ge(a_sum, r + 1)
                p, rp = powers(asum[h][:, :], h, 2, r if r < LOADS - 1 else r + 1)
                nc.vector.tensor_scalar(ascale[h][:, :], rp, PART, None, ALU.mult).then_inc(a_scale, 1)
                nc.vector.tensor_scalar(aback[:, 2 * r:2 * r + 2], p, 1.0 / PART, None, ALU.mult)
                nc.vector.tensor_scalar(abackb[:, 2 * r:2 * r + 2], p, 1.0 / PART, None, ALU.mult)

            def adjacency_lo(r):
                for v in range(2):
                    k = 2 * r + v
                    dve.wait_ge(at_hi, k + 1)
                    nc.vector.scalar_tensor_tensor(ATl[:, k, :], stage[r % 2][:, v, :], ascale[r % 2][:, v:v + 1],
                                                   ATh[:, k, :], ALU.mult, ALU.subtract).then_inc(at_lo, 1)

            def next_factors(n):
                if n < 2 * LOADS:
                    if n:
                        dve.wait_ge(xn_done, 2 * n)
                    factors(n, slice(0, 2))

            column_scales(0)
            adjacency_lo(0)
            dve.wait_ge(w_in0, 16)
            nc.vector.tensor_tensor(w0_in[:, 0, :], w0_in[:, 0, :], w0_in[:, 2, :], ALU.subtract).then_inc(w_combined, 1)
            nc.vector.tensor_scalar(w0_in[:, 2, :], w0_in[:, 2, :], 2.0, None, ALU.mult).then_inc(w_combined, 1)
            weights_maximum(0)
            column_scales(1)
            pair_statistics(0)
            next_factors(0)
            adjacency_lo(1)
            column_scales(2)
            weights_scale(0)
            pair_statistics(1)
            adjacency_lo(2)
            weights_lo(0)
            transposed_lo(0, 0)
            column_scales(3)
            transposed_lo(1, 1)
            next_factors(1)
            adjacency_lo(3)
            pair_statistics(2)
            next_factors(2)
            for r in range(1, 2 * LOADS + 1):
                def finish(v):
                    t = 2 * (r - 1) + v
                    z, m = (t // M, t % M) if t >= EARLY else (None, None)
                    first_columns(t, t, 0, z, m)

                def transposed(v):
                    if r < 2 * LOADS:
                        transposed_lo(2 * r + v, v)

                finish(0)
                if r == 1:
                    degree_factors()
                if r == 2:
                    next_factors(3)
                transposed(0)
                if r == LOADS + 1:
                    for m in range(2):
                        evacuate(0, m, m)
                elif r > LOADS + 1:
                    evacuate(0, r - LOADS, (r - LOADS) % 2)
                if 1 < r < 2 * LOADS - 2:
                    pair_rows(r + 2)
                if r == 1:
                    layer_scale(0)
                finish(1)
                transposed(1)
                if r == 1:
                    for m in range(EARLY):
                        split_lo_tile(0, m)
                    pair_statistics(r + 2)
                elif r < 2 * LOADS - 2:
                    pair_moments(r + 2)
                if r > 1:
                    next_factors(r + 2)
            dve.wait_ge(w_in1, 16)
            nc.vector.tensor_tensor(w1_in[:, 1:4, :], w1_in[:, 1:4, :], w1_in[:, 4:7, :], ALU.add).then_inc(w_combined, 1)
            weights_maximum(1)
            weights_scale(1)
            weights_lo(1)
            for m in range(LOADS + 1, M):
                evacuate(0, m, m % 2)
            half_maximum(2)
            evacuate(1, 0, 0)
            half_scale(2)
            split_lo(2, 0, M // 2)
            evacuate(1, 1, 1)
            split_lo(2, M // 2, M // 2)
            with dve.Fori(1, LOADS) as i:
                for u in range(2):
                    evacuate(1, 2 * i + u, u)
            layer_scale(1)
            half_maximum(3)

            def follow(c, m, u, last=False):
                j = m - 1 + J1 + c * M
                transposed_lo(j, 1 - u)
                evacuate(2 + c, m, u)
                dve.wait_ge(bank_free, m + (2 + c) * M + 3)
                statistics(j + 1 - J1 + 2 * LOADS, [(m + c * M, u)], u)
                factors(j + 1 - J1 + 2 * LOADS, u)
                if c == 0:
                    split_lo_tile(3, m)
                if c == 1 and last:
                    nc.vector.tensor_copy(ATl_diag, ADl[:, :, :]).then_inc(diag_lo, 1)
                first_columns(j, m - 1 + c * M, 1, (4 + c) % 3, m - 1)

            for c in range(2):
                g0 = (2 + c) * M
                if c == 0:
                    evacuate(2, 0, 0)
                    dve.wait_ge(bank_free, g0 + 3)
                    statistics(2 * LOADS, [(0, 0)], 0)
                    factors(2 * LOADS, 0)
                    half_scale(3)
                    split_lo_tile(3, 0)
                else:
                    transposed_lo(J1 + M - 1, 1)
                    evacuate(3, 0, 0)
                    dve.wait_ge(bank_free, g0 + 3)
                    statistics(2 * LOADS + M, [(M, 0)], 0)
                    factors(2 * LOADS + M, 0)
                    first_columns(J1 + M - 1, M - 1, 1, 1, M - 1)
                with dve.Fori(0, LOADS - 1) as i:
                    follow(c, 2 * i + 1, 1)
                    follow(c, 2 * i + 2, 0)
                follow(c, M - 1, 1, last=True)
            transposed_lo(J1 + 2 * M - 1, 1)
            evacuate(4, 0, 0)
            first_columns(J1 + 2 * M - 1, 2 * M - 1, 1, 2, M - 1)
            with dve.Fori(0, LOADS - 1) as i:
                evacuate(4, 2 * i + 1, 1)
                evacuate(4, 2 * i + 2, 0)
            evacuate(4, M - 1, 1)
            for q in range(5, 10):
                if q < 9:
                    half_maximum(q + 1)
                evacuate(q, 0, 0)
                if q < 9:
                    half_scale(q + 1)
                    split_lo(q + 1, 0, M // 2)
                evacuate(q, 1, 1)
                if q < 9:
                    split_lo(q + 1, M // 2, M // 2)
                with dve.Fori(1, LOADS) as i:
                    for u in range(2):
                        evacuate(q, 2 * i + u, u)


_INS = ["x", "adj", "L0_gnn_Ws", "L0_gnn_bias", "L1_gnn_weight_1"]


def kernel(**inputs):
    import numpy as _np
    import concourse.bacc as _bacc
    from concourse import mybir as _mybir
    from concourse.bass_utils import run_bass_kernel_spmd as _run

    nc = _bacc.Bacc("TRN2", target_bir_lowering=False, num_devices=1)
    a = {n: _np.asarray(inputs[n]) for n in _INS}
    B, N, F = a["x"].shape
    a["x"] = a["x"].reshape(2, B // 2, N // P, P, F).transpose(0, 2, 3, 1, 4).reshape(2 * N // P, P, B // 2 * F)
    a["adj"] = a["adj"].T
    a["L1_gnn_weight_1"] = a["L1_gnn_weight_1"].transpose(2, 0, 1)
    arrays, args = {}, []
    for name in _INS:
        v = _np.ascontiguousarray(a[name])
        arrays[f"in_{name}_dram"] = v
        args.append(nc.dram_tensor(f"in_{name}_dram", v.shape, _mybir.dt.from_np(v.dtype), kind="ExternalInput").ap())
    shape = arrays["in_x_dram"].shape
    args.append(nc.dram_tensor("out_0_dram", shape, _mybir.dt.float32, kind="ExternalOutput").ap())
    build(nc, *args)
    r = _run(nc, [arrays], core_ids=[0])
    y = r.results[0]["out_0_dram"].reshape(2, N // P, P, B // 2, F)
    return _np.ascontiguousarray(y.transpose(0, 3, 1, 2, 4).reshape(B, N, F))
```
